# Optimizing a Trainium2 kernel written in Bass

```python
import numpy as np
import jax
import jax.numpy as jnp

def _softmax(x, axis=-1):
    return jax.nn.softmax(x, axis=axis)

def _gelu(x):
    return jax.nn.gelu(x, approximate=True)

def _silu(x):
    return jax.nn.silu(x)

def _sigmoid(x):
    return jax.nn.sigmoid(x)

def _layernorm(x, axis=-1, eps=1e-05):
    m = jnp.mean(x, axis=axis, keepdims=True)
    v = jnp.var(x, axis=axis, keepdims=True)
    return (x - m) / jnp.sqrt(v + eps)

def _scatter_add(tgt, idx, src, axis=0):
    return tgt.at[idx].add(src)

def _segment_sum(src, seg, n):
    return jax.ops.segment_sum(src, seg, n)
kernel_name = 'mk_flamingo_gated_d1_seqx_r8_4ef6cb'

def setup_inputs(seed: int=0):
    np.random.seed(seed)
    _w = jnp.asarray

    def _rec_inputs():
        import jax
        import jax.numpy as jnp
        _rk = jax.random.key(seed)
        x = -0.0002928 + 1 * jax.random.normal(jax.random.fold_in(_rk, 1), (32, 128, 128), jnp.float32)
        _lenS = 128 - jax.random.randint(jax.random.fold_in(_rk, 7), (32,), 0, max(1, 128 // 4) + 1, jnp.int32)
        _lenS2 = 120 - jax.random.randint(jax.random.fold_in(_rk, 8), (32,), 0, max(1, 120 // 4) + 1, jnp.int32)
        _ctx_1024P = jax.random.normal(jax.random.fold_in(_rk, 11), (32, 16, 128), jnp.float32)
        _ctx_1024c = jax.random.dirichlet(jax.random.fold_in(_rk, 511), 0.3 * jnp.ones((16,), jnp.float32), (32, 120))
        _ctx_1024t = jnp.einsum('bsk,bkd->bsd', _ctx_1024c, _ctx_1024P)
        _ctx_1024t = _ctx_1024t * jax.lax.rsqrt(jnp.mean(jnp.square(_ctx_1024t)) + 1e-12) * 0.953939
        ctx_1024 = -1.39393e-06 + 0.999914 * (_ctx_1024t + 0.3 * jax.random.normal(jax.random.fold_in(_rk, 611), (32, 120, 128), jnp.float32))
        _validS = jnp.arange(128)[None, :] < _lenS[:, None]
        _validS2 = jnp.arange(120)[None, :] < _lenS2[:, None]
        _causal = jnp.tril(jnp.ones((128, 128), dtype=bool))
        mask_Bx1x1xS2_ik0 = jnp.where(jnp.broadcast_to(_validS2[:, None, None, :], (32, 1, 1, 120)), 0, 1).astype(jnp.int32)
        _g = jax.random.normal(jax.random.fold_in(_rk, 9001), (2, 1), jnp.float32)
        _g = jnp.sign(_g) * jnp.maximum(jnp.abs(_g), 1.0) + (_g == 0) * 1.0
        g_xattn = _g[0]
        g_ffn = _g[1]
        return (x, ctx_1024, mask_Bx1x1xS2_ik0, g_xattn, g_ffn)
    x, ctx_1024, mask_Bx1x1xS2_ik0, g_xattn, g_ffn = _rec_inputs()

    def _L0_xattn_setup():
        import jax, jax.numpy as jnp
        import numpy as np
        EMBED_DIM = 128
        NUM_HEADS = 16
        HEAD_DIM = EMBED_DIM // NUM_HEADS
        key = jax.random.key(seed)
        ks = jax.random.split(key, 10)
        B, Sq, Skv, D = (2, 256, 256, EMBED_DIM)
        query = jax.random.normal(ks[0], (B, Sq, D), dtype=jnp.float32)
        k_in = jax.random.normal(ks[1], (B, Skv, D), dtype=jnp.float32)
        v_in = jax.random.normal(ks[2], (B, Skv, D), dtype=jnp.float32)
        mask = jax.random.randint(ks[3], (B, 1, 1, Skv), 0, 2, dtype=jnp.int32)
        mask = mask.at[..., 0].set(1)
        s = 1.0 / np.sqrt(D)
        Wq = jax.random.normal(ks[4], (D, D), dtype=jnp.float32) * s
        Wk = jax.random.normal(ks[5], (D, D), dtype=jnp.float32) * s
        Wv = jax.random.normal(ks[6], (D, D), dtype=jnp.float32) * s
        bq = jax.random.normal(ks[7], (D,), dtype=jnp.float32) * 0.01
        bk = jax.random.normal(ks[8], (D,), dtype=jnp.float32) * 0.01
        bv = jax.random.normal(ks[9], (D,), dtype=jnp.float32) * 0.01
        return {'query': query, 'key': k_in, 'value': v_in, 'mask': mask, 'Wq': Wq, 'bq': bq, 'Wk': Wk, 'bk': bk, 'Wv': Wv, 'bv': bv}
    _L0_xattn_all = _L0_xattn_setup()
    _L0_xattn_in = {k: v for k, v in _L0_xattn_all.items() if k in ('Wq', 'bq', 'Wk', 'bk', 'Wv', 'bv')}
    del _L0_xattn_all

    def _L0_ffn_setup():
        import jax, jax.numpy as jnp
        import numpy as np
        EPS = 1e-08

        def _ternary_linear(x, w):
            alpha = jnp.mean(jnp.abs(w))
            w_t = jnp.sign(w) * (jnp.abs(w) > 0.5 * alpha).astype(w.dtype)
            w_q = w + jax.lax.stop_gradient(w_t - w)
            d = x.shape[-1]
            rms = jnp.sqrt(jnp.sum(x * x, axis=-1, keepdims=True)) / jnp.sqrt(jnp.asarray(d, x.dtype))
            x_norm = x / (rms + EPS)
            return jnp.einsum('bsd,fd->bsf', x_norm, w_q)
        key = jax.random.key(seed)
        k1, k2, k3 = jax.random.split(key, 3)
        d_model, d_ff = (128, 512)
        B, S = (4, 512)
        x = jax.random.normal(k1, (B, S, d_model), dtype=jnp.float32)
        w_up = jax.random.normal(k2, (d_ff, d_model), dtype=jnp.float32) * 0.02
        w_down = jax.random.normal(k3, (d_model, d_ff), dtype=jnp.float32) * 0.02
        return {'x': x, 'w_up': w_up, 'w_down': w_down}
    _L0_ffn_all = _L0_ffn_setup()
    _L0_ffn_in = {k: v for k, v in _L0_ffn_all.items() if k in ('w_up', 'w_down')}
    del _L0_ffn_all
    return {'x': x, 'ctx_1024': ctx_1024, 'mask_Bx1x1xS2_ik0': mask_Bx1x1xS2_ik0, 'g_xattn': g_xattn, 'g_ffn': g_ffn, 'L0_xattn_Wq': _L0_xattn_in['Wq'], 'L0_xattn_bq': _L0_xattn_in['bq'], 'L0_xattn_Wk': _L0_xattn_in['Wk'], 'L0_xattn_bk': _L0_xattn_in['bk'], 'L0_xattn_Wv': _L0_xattn_in['Wv'], 'L0_xattn_bv': _L0_xattn_in['bv'], 'L0_ffn_w_up': _L0_ffn_in['w_up'], 'L0_ffn_w_down': _L0_ffn_in['w_down']}

def reference(x, ctx_1024, mask_Bx1x1xS2_ik0, g_xattn, g_ffn, L0_xattn_Wq, L0_xattn_bq, L0_xattn_Wk, L0_xattn_bk, L0_xattn_Wv, L0_xattn_bv, L0_ffn_w_up, L0_ffn_w_down):
    import jax
    import jax.numpy as jnp

    def _L0_xattn_ref(query, key, value, mask, Wq, bq, Wk, bk, Wv, bv):
        import jax, jax.numpy as jnp
        import numpy as np
        EMBED_DIM = 128
        NUM_HEADS = 16
        HEAD_DIM = EMBED_DIM // NUM_HEADS
        B, Sq, D = query.shape
        Skv = key.shape[1]
        H, hd = (NUM_HEADS, HEAD_DIM)
        Q = (query @ Wq.T + bq).reshape(B, Sq, H, hd).transpose(0, 2, 1, 3)
        K = (key @ Wk.T + bk).reshape(B, Skv, H, hd).transpose(0, 2, 1, 3)
        V = (value @ Wv.T + bv).reshape(B, Skv, H, hd).transpose(0, 2, 1, 3)
        scale = jnp.sqrt(jnp.asarray(hd, dtype=jnp.float32))
        scores = jnp.einsum('bhqd,bhkd->bhqk', Q, K) / scale
        scores = jnp.where(mask == 0, -jnp.inf, scores)
        attn = jax.nn.softmax(scores, axis=-1)
        out = jnp.einsum('bhqk,bhkd->bhqd', attn, V)
        out = out.transpose(0, 2, 1, 3).reshape(B, Sq, H * hd)
        return out

    def _L0_ffn_ref(x, w_up, w_down):
        import jax, jax.numpy as jnp
        import numpy as np
        EPS = 1e-08

        def _ternary_linear(x, w):
            alpha = jnp.mean(jnp.abs(w))
            w_t = jnp.sign(w) * (jnp.abs(w) > 0.5 * alpha).astype(w.dtype)
            w_q = w + jax.lax.stop_gradient(w_t - w)
            d = x.shape[-1]
            rms = jnp.sqrt(jnp.sum(x * x, axis=-1, keepdims=True)) / jnp.sqrt(jnp.asarray(d, x.dtype))
            x_norm = x / (rms + EPS)
            return jnp.einsum('bsd,fd->bsf', x_norm, w_q)
        h = jax.nn.gelu(_ternary_linear(x, w_up), approximate=False)
        return _ternary_linear(h, w_down)
    x = x + jnp.tanh(g_xattn[0]) * _L0_xattn_ref(_layernorm(x, axis=-1), ctx_1024, ctx_1024, mask_Bx1x1xS2_ik0, L0_xattn_Wq, L0_xattn_bq, L0_xattn_Wk, L0_xattn_bk, L0_xattn_Wv, L0_xattn_bv)
    x = x + jnp.tanh(g_ffn[0]) * _L0_ffn_ref(_layernorm(x, axis=-1), L0_ffn_w_up, L0_ffn_w_down)
    return x

_drawn_inputs = setup_inputs


def setup_inputs(seed=0):
    import zlib

    import numpy as np

    out = dict(_drawn_inputs(seed))
    spreads = {}
    factors = {'L0_xattn_bq': 25.237, 'L0_xattn_bk': 64.0, 'L0_xattn_bv': 7.142}
    for name, (base, spread) in spreads.items():
        noise = np.random.default_rng([zlib.crc32(name.encode()), seed]).standard_normal(out[name].shape)
        drawn = base * np.exp(spread * noise) if base else spread * noise
        out[name] = jnp.asarray(drawn.astype(out[name].dtype))
    for name, factor in factors.items():
        out[name] = (out[name] * factor).astype(out[name].dtype)
    return out
```

```python
from contextlib import ExitStack

import concourse.bass as bass
from concourse import mybir

F32 = mybir.dt.float32
F32R = mybir.dt.float32r
I32 = mybir.dt.int32
ALU = mybir.AluOpType
ACT = mybir.ActivationFunctionType
AX = mybir.AxisListType

B, S, D = 32, 128, 128
KV = 120
H, HD = 16, 8
F = 512
NB = 4
QUADS = B // NB
G, J = 4, 4
C = 4
FC = F // 128
LN_EPS = 1e-5
RMS_EPS = 1e-8
SCALE = float(HD) ** -0.5
VC = 32
NT = 3 * G + 1


def flamingo_kernel(nc, x, context, mask, g_xattn, g_ffn, wq, bq, wk, bk, wv, bv, w_up, w_down, out):
    ctx = ExitStack()
    with ctx:
        def sb(name, shape, dt=F32):
            return ctx.enter_context(nc.sbuf_tensor(name, shape, dt))

        def psum(name, shape):
            return ctx.enter_context(nc.psum_tensor(name, shape, F32))

        def sem(name):
            return ctx.enter_context(nc.semaphore(name))

        xs = sb("xs", [S, B + 1, D])
        ident = sb("ident", [128, 128])
        ident_r = sb("ident_r", [128, 128], F32R)
        ones = sb("ones", [128, 128])
        select = {n: sb(n, [128, G, 128], F32R) for n in ("q_hi_sel", "q_lo_sel", "k_hi_sel", "k_lo_sel")}
        w_raw = sb("w_raw", [128, 3, D])
        w_t = sb("w_t", [128, 3, D])
        q_bias = sb("q_bias", [128, 1])
        k_bias = sb("k_bias", [128, 1])
        v_bias = sb("v_bias", [128, D])
        gates = sb("gates", [128, 2])
        tanh_g = sb("tanh_g", [128, 2])
        gated_bias = sb("gated_bias", [128, D])
        mask_rows = sb("mask_rows", [B, KV], I32)
        mask_rows_f = sb("mask_rows_f", [B, KV])
        valid = sb("valid", [KV, B])
        valid_n = sb("valid_n", [KV, B])
        valid_share = sb("valid_share", [KV, B])
        minus_half = sb("minus_half", [128, B + 1])
        half = sb("half", [128, B + 1])

        context_in = sb("context_in", [KV, 2, NB, D])
        mask_in = sb("mask_in", [KV, NB * KV], I32)
        invalid = sb("invalid", [KV, NB, KV])
        diag = sb("diag", [KV, NB, KV])
        fill = sb("fill", [KV, NB, KV])
        stats = sb("stats", [S, NB, 6])
        moments = sb("moments", [S, NB, 2])
        var_eps = sb("var_eps", [S, NB])
        rstd = sb("rstd", [S, NB])
        xn = sb("xn", [S, NB, D])
        xn_t = sb("xn_t", [D, NB * S])
        context_t = sb("context_t", [D, NB, KV])
        q_hi = sb("q_hi", [128, NB * S], F32R)
        q_lo = sb("q_lo", [128, NB * S], F32R)
        k_hi = sb("k_hi", [128, NB * KV], F32R)
        k_lo = sb("k_lo", [128, NB * KV], F32R)
        q_rows = sb("q_rows", [128, G, NB * S], F32R)
        q_slots = [sb(f"q_slots{p}", [128, G, J, NB, S], F32R) for p in range(2)]
        k_rows = [sb(f"k_rows{p}", [128, G, NB, KV], F32R) for p in range(2)]
        v_store = [sb(f"v_blocks{p}", [128, NB, H, VC]) for p in range(2)]
        v_blocks = [v[0:KV] for v in v_store]
        neg_max = sb("neg_max", [S, 2, H], F32R)
        p_store = sb("probs", [128, G, J, S])
        probs = p_store[0:KV]
        att_t = sb("att_t", [128, 2, S])
        inv_den = sb("inv_den", [S, H])
        att = sb("att", [S, D])
        stats2 = sb("stats2", [S, B + 1, 2, 3])
        mean2 = sb("mean2", [S, B + 1])
        mean_gap = sb("mean_gap", [S, B + 1])
        var2 = sb("var2", [S, B + 1])
        root = sb("root", [S, B + 1])
        var2_eps = sb("var2_eps", [S, B + 1])
        root_eps = sb("root_eps", [S, B + 1])
        ffn_den = sb("ffn_den", [S, B + 1])
        ffn_scale = sb("ffn_scale", [S, B + 1])

        wu_raw = sb("wu_raw", [128, FC, D])
        wd_raw = sb("wd_raw", [D, F])
        tern = sb("tern", [128, 2, F])
        tern_neg = sb("tern_neg", [128, 2, F])
        abs_sum = sb("abs_sum", [128, 2])
        thresh = sb("thresh", [128, 2])
        neg_thresh = sb("neg_thresh", [128, 2])
        wu_t = sb("wu_t", [D, F])
        wd_t = sb("wd_t", [128, FC, D])
        y = sb("y", [S, NB, D])
        y_t = sb("y_t", [D, NB * S])
        act_h = [v[:].rearrange("p b h c -> p (b h c)").rearrange("p (c n) -> p c n", c=FC) for v in v_store]
        squares = p_store[:].rearrange("p g j s -> p g (j s)")
        square_sum = sb("square_sum", [128, NB * S])
        mean_sq = sb("mean_sq", [S, NB])
        rms = sb("rms", [S, NB])
        rms_inv = sb("rms_inv", [S, NB])
        out_scale = sb("out_scale", [S, NB])

        ps_s = [psum(f"ps_s{i}", [128, 512]) for i in range(2)]
        ps_st = [psum(f"ps_st{i}", [128, 512]) for i in range(2)]
        ps_o = psum("ps_o", [128, 512])
        ps_t = psum("ps_t", [128, 512])
        ps_p = [psum(f"ps_p{i}", [128, 512]) for i in range(2)]

        ld_x = [sem(f"ld_x{p}") for p in range(2)]
        ld_w = sem("ld_w")
        ld_small = sem("ld_small")
        ld_ctx = [sem(f"ld_ctx{p}") for p in range(2)]
        ld_mask = sem("ld_mask")
        ld_ffn = sem("ld_ffn")
        ident_zero = sem("ident_zero")
        ident_ok = sem("ident_ok")
        ident_r_ok = sem("ident_r_ok")
        const_ok = sem("const_ok")
        sel_zero = sem("sel_zero")
        sel_ok = sem("sel_ok")
        pad_ok = sem("pad_ok")
        tanh_ok = sem("tanh_ok")
        gbias_ok = sem("gbias_ok")
        wt_ps = sem("wt_ps")
        wt_ok = sem("wt_ok")
        maskf_ok = sem("maskf_ok")
        maskt_ps = sem("maskt_ps")
        valid_ok = sem("valid_ok")
        count_ps = sem("count_ps")
        count_ok = sem("count_ok")
        share_ok = sem("share_ok")
        stats_ok = sem("stats_ok")
        moments_ok = sem("moments_ok")
        vareps_ok = sem("vareps_ok")
        rstd_ok = sem("rstd_ok")
        xn_ok = sem("xn_ok")
        xb_ok = sem("xb_ok")
        invalid_ok = sem("invalid_ok")
        diag_ok = sem("diag_ok")
        fill_ok = sem("fill_ok")
        xt_ps = sem("xt_ps")
        xt_ok = sem("xt_ok")
        ct_ps = sem("ct_ps")
        ct_ok = sem("ct_ok")
        q_ps = sem("q_ps")
        qhi_ok = sem("qhi_ok")
        qlo_ok = sem("qlo_ok")
        k_ps = sem("k_ps")
        khi_ok = sem("khi_ok")
        klo_ok = sem("klo_ok")
        v_ps = sem("v_ps")
        v_ok = sem("v_ok")
        qrows_ps = sem("qrows_ps")
        qrows_ok = sem("qrows_ok")
        qslots_ok = sem("qslots_ok")
        krows_ps = sem("krows_ps")
        krows_ok = sem("krows_ok")
        s_ps = sem("s_ps")
        max_ok = sem("max_ok")
        st_ps = sem("st_ps")
        exp_ok = sem("exp_ok")
        o_ps = sem("o_ps")
        o_ok = sem("o_ok")
        t_ps = sem("t_ps")
        den_ok = sem("den_ok")
        att_ok = sem("att_ok")
        x2_ok = sem("x2_ok")
        stats2_ok = sem("stats2_ok")
        moments2_ok = sem("moments2_ok")
        gap_ok = sem("gap_ok")
        root_ok = sem("root_ok")
        den2_ok = sem("den2_ok")
        scale2_ok = sem("scale2_ok")
        abs_ok = sem("abs_ok")
        abs_ps = sem("abs_ps")
        thresh_ok = sem("thresh_ok")
        neg_ok = sem("neg_ok")
        tern_ok = sem("tern_ok")
        ternt_ps = sem("ternt_ps")
        ternt_ok = sem("ternt_ok")
        y_ok = sem("y_ok")
        yt_ps = sem("yt_ps")
        yt_ok = sem("yt_ok")
        up_ps = sem("up_ps")
        gelu_ok = sem("gelu_ok")
        sq_ok = sem("sq_ok")
        sqsum_ok = sem("sqsum_ok")
        down_ps = sem("down_ps")
        ssq_ps = sem("ssq_ps")
        meansq_ok = sem("meansq_ok")
        rms_ok = sem("rms_ok")
        rmse_ok = sem("rmse_ok")
        rinv_ok = sem("rinv_ok")
        oscale_ok = sem("oscale_ok")
        res_ok = sem("res_ok")
        st_out = sem("st_out")

        EXP0, O0, X20, GELU0 = 2, 1, 1, FC

        up_banks = ps_s + ps_st

        block = ctx.enter_context(nc.Block())

        def quads(eng, step):
            with eng.Fori(0, QUADS // 2 - 1) as it:
                for par in range(2):
                    step(it, par, 2)
            step(QUADS // 2 - 1, 0, 1)
            step(QUADS // 2 - 1, 1, 0)

        @block.sync
        def _(sp):
            def load_x(q, par):
                sp.dma_start(xs[:, bass.ds(q * NB + 1, NB), :], x[bass.ds(q * NB, NB)].rearrange("b s d -> s b d")) \
                    .then_inc(ld_x[par], 16)

            load_x(0, 0)
            sp.dma_start(mask_in[:], mask[0:NB].rearrange("b k -> (b k)").rearrange("(o n) -> o n", o=1)
                         .to_broadcast([KV, NB * KV])).then_inc(ld_mask, 16)
            sp.dma_start(mask_rows[:], mask).then_inc(ld_small, 16)
            for n, w in enumerate((wq, wk, wv)):
                sp.dma_start(w_raw[:, n, :], w).then_inc(ld_w, 16)

            def load_context(q, par):
                sp.dma_start(context_in[:, par], context[bass.ds(q * NB, NB)].rearrange("b k d -> k b d")) \
                    .then_inc(ld_ctx[par], 16)

            def load_mask(q):
                sp.dma_start(mask_in[:], mask[bass.ds(q * NB, NB)].rearrange("b k -> (b k)")
                             .rearrange("(o n) -> o n", o=1).to_broadcast([KV, NB * KV])).then_inc(ld_mask, 16)

            load_context(0, 0)
            sp.dma_start(q_bias[:], bq.rearrange("(p o) -> p o", o=1)).then_inc(ld_small, 16)
            sp.dma_start(k_bias[:], bk.rearrange("(p o) -> p o", o=1)).then_inc(ld_small, 16)
            sp.dma_start(v_bias[:], bv.rearrange("(o n) -> o n", o=1).to_broadcast([128, D])).then_inc(ld_small, 16)
            for n, g in enumerate((g_xattn, g_ffn)):
                sp.dma_start(gates[:, n:n + 1], g.rearrange("(o n) -> o n", o=1).to_broadcast([128, 1])) \
                    .then_inc(ld_small, 16)
            load_context(1, 1)
            load_x(1, 1)
            sp.wait_ge(invalid_ok, 1)
            load_mask(1)
            sp.dma_start(wu_raw[:], w_up.rearrange("(c p) d -> p c d", p=128)).then_inc(ld_ffn, 16)
            sp.dma_start(wd_raw[:], w_down).then_inc(ld_ffn, 16)

            def spread_q(q, par):
                sp.wait_ge(qrows_ok, G * (q + 1))
                for j in range(J):
                    sp.dma_start(q_slots[par][32 * j:32 * j + 32, :, j].rearrange("p g b s -> p g (b s)").bitcast(F32),
                                 q_rows[32 * j:32 * j + 32, :, :].bitcast(F32)).then_inc(qslots_ok, 16)

            sp.wait_ge(pad_ok, 1)
            spread_q(0, 0)

            def step(k, par, ahead):
                q = 2 * k + par
                if ahead == 2:
                    sp.wait_ge(invalid_ok, q + 2)
                    load_mask(q + 2)
                    sp.wait_ge(ct_ps, q + 1)
                    load_context(q + 2, par)
                    load_x(q + 2, par)
                if ahead:
                    spread_q(q + 1, 1 - par)

            quads(sp, step)

            with sp.Fori(0, QUADS) as q:
                sp.wait_ge(res_ok, NB * (q + 1) + 1)
                sp.dma_start(out[bass.ds(q * NB, NB)].rearrange("b s d -> s b d"),
                             xs[:, bass.ds(q * NB + 1, NB), :]).then_inc(st_out, 16)
            sp.wait_ge(st_out, 16 * QUADS)

        @block.gpsimd
        def _(pool):
            pool.memset(ident[:], 0.0).then_inc(ident_zero, 1)
            pool.wait_ge(ident_zero, 1)
            pool.affine_select(out=ident[:], in_=ident[:], compare_op=ALU.not_equal, fill=1.0, base=0,
                               pattern=[[-1, 128]], channel_multiplier=1).then_inc(ident_ok, 1)
            pool.memset(minus_half[:], -0.5).then_inc(const_ok, 1)
            pool.memset(half[:], 0.5).then_inc(const_ok, 1)
            pool.memset(ones[:], 1.0).then_inc(const_ok, 1)
            pool.memset(v_blocks[0], 0.0).then_inc(const_ok, 1)
            pool.memset(q_slots[0][:].bitcast(F32), 0.0).then_inc(pad_ok, 1)

            def ahead_of(q):
                pool.wait_ge(fill_ok, NB * q + 1)
                for b in range(NB):
                    pool.tensor_tensor(diag[:, b, :], ident[0:KV, 0:KV],
                                       valid[:, bass.ds(q * NB + b, 1)].to_broadcast([KV, KV]), ALU.mult) \
                        .then_inc(diag_ok, 1)
                pool.wait_ge(vareps_ok, q + 1)
                pool.tensor_tensor(rstd[:], var_eps[:], minus_half[:, 0:NB], ALU.pow).then_inc(rstd_ok, 1)
                pool.wait_ge(xn_ok, NB * (q + 1))
                pool.tensor_tensor(xs[:, bass.ds(q * NB + 1, NB), :], xs[:, bass.ds(q * NB + 1, NB), :],
                                   gated_bias[:].rearrange("p (o n) -> p o n", o=1).to_broadcast([S, NB, D]),
                                   ALU.add).then_inc(xb_ok, 1)

            pool.wait_ge(gbias_ok, 1)
            pool.wait_ge(valid_ok, 1)
            pool.memset(v_blocks[1], 0.0).then_inc(const_ok, 1)
            ahead_of(0)
            pool.memset(q_slots[1][:].bitcast(F32), 0.0).then_inc(pad_ok, 1)
            ahead_of(1)

            def step(k, par, ahead):
                if ahead == 2:
                    ahead_of(2 * k + par + 2)

            quads(pool, step)

            pool.wait_ge(moments2_ok, 4)
            pool.tensor_tensor(root[:], var2[:], half[:], ALU.pow).then_inc(root_ok, 1)
            pool.wait_ge(moments2_ok, 5)
            pool.tensor_tensor(root_eps[:], var2_eps[:], half[:], ALU.pow).then_inc(root_ok, 1)

            def ffn(q, par):
                for c in range(FC):
                    pool.wait_ge(gelu_ok, GELU0 + FC * q + c + 1)
                    if c == 0:
                        pool.wait_ge(sqsum_ok, q + 1)
                    pool.tensor_tensor(squares[:, c, :], act_h[par][:, c, :], act_h[par][:, c, :], ALU.mult) \
                        .then_inc(sq_ok, 1)
                pool.wait_ge(meansq_ok, q + 1)
                pool.tensor_tensor(rms[:], mean_sq[:], half[:, 0:NB], ALU.pow).then_inc(rms_ok, 1)

            with pool.Fori(0, QUADS // 2) as it:
                for par in range(2):
                    ffn(2 * it + par, par)

        @block.scalar
        def _(act):
            act.wait_ge(ld_small, 16 * 6)
            act.activation(tanh_g[:], gates[:], ACT.Tanh).then_inc(tanh_ok, 1)
            for n in range(3):
                act.wait_ge(wt_ps, n + 1)
                act.activation(w_t[:, n, :], ps_s[n % 2][:, 0:D], ACT.Copy).then_inc(wt_ok, 1)

            def evacuate(task, q, par, first=False):
                bank = ps_p[task % 2]
                if task == 0:
                    act.wait_ge(xt_ps, q + 1)
                    act.activation(xn_t[:], bank[:], ACT.Copy).then_inc(xt_ok, 1)
                elif task == 2:
                    act.wait_ge(q_ps, q + 1)
                    act.activation(q_hi[:], bank[:], ACT.Identity, bias=q_bias[:, 0:1]).then_inc(qhi_ok, 1)
                elif task == 3:
                    act.wait_ge(k_ps, q + 1)
                    act.activation(k_hi[:], bank[:, 0:NB * KV], ACT.Identity, bias=k_bias[:, 0:1]) \
                        .then_inc(khi_ok, 1)
                elif 4 <= task < 8:
                    g = task - 4
                    act.wait_ge(qrows_ps, G * q + g + 1)
                    if g == 0 and not first:
                        act.wait_ge(qslots_ok, 16 * J * q)
                    act.activation(q_rows[:, g, :], bank[:], ACT.Copy).then_inc(qrows_ok, 1)

            for task in range(NT):
                evacuate(task, 0, 0, first=True)
            act.activation(att_t[:], ident[:, 0:1].to_broadcast([128, 2 * S]).rearrange("p (a b) -> p a b", a=2),
                           ACT.Identity, bias=1.0, scale=0.0).then_inc(o_ok, O0)

            def step(k, par, ahead):
                q = 2 * k + par
                for b in range(NB):
                    t = NB * q + b
                    for g in range(G):
                        act.wait_ge(st_ps, G * t + g + 1)
                        act.activation(probs[:, g].rearrange("p j s -> p (j s)"), ps_st[g % 2][0:KV, :], ACT.Exp,
                                       scale=SCALE).then_inc(exp_ok, 1)
                        if ahead and b < 3:
                            evacuate(G * b + g, q + 1, 1 - par)
                    act.wait_ge(o_ps, t + 1)
                    act.activation(att_t[:].rearrange("p a s -> p (a s)"), ps_o[:, 0:2 * S], ACT.Copy) \
                        .then_inc(o_ok, 1)

            quads(act, step)

            for c in range(2 * FC):
                act.wait_ge(ternt_ps, c + 1)
                dst = wu_t[:, c * 128:(c + 1) * 128] if c < FC else wd_t[:, c - FC, :]
                act.activation(dst, ps_s[c % 2][:, 0:128], ACT.Copy).then_inc(ternt_ok, 1)

            def ffn(q, par):
                act.wait_ge(yt_ps, q + 1)
                act.activation(y_t[:], ps_p[0][:], ACT.Copy).then_inc(yt_ok, 1)
                for c in range(FC):
                    act.wait_ge(up_ps, FC * q + c + 1)
                    act.activation(act_h[par][:, c, :], up_banks[c][:], ACT.Gelu).then_inc(gelu_ok, 1)

            with act.Fori(0, QUADS // 2) as it:
                for par in range(2):
                    ffn(2 * it + par, par)

        @block.tensor
        def _(pe):
            pe.wait_ge(ident_ok, 1)
            for n in range(3):
                pe.wait_ge(ld_w, 48)
                if n == 2:
                    pe.wait_ge(wt_ok, 1)
                pe.transpose(ps_s[n % 2][:, 0:D], w_raw[:, n, :], ident[:]).then_inc(wt_ps, 1)
            pe.wait_ge(maskf_ok, 1)
            pe.transpose(ps_o[0:KV, 0:B], mask_rows_f[:], ident[0:B, 0:B]).then_inc(maskt_ps, 1)
            pe.wait_ge(valid_ok, 1)
            pe.wait_ge(const_ok, 3)
            pe.matmul(ps_t[0:KV, 0:B], ones[0:KV, 0:KV], valid[:], start=True, stop=True).then_inc(count_ps, 1)
            pe.wait_ge(wt_ok, 3)

            def prepare(task, k, par, first=False):
                q = 2 * k + par
                bank = ps_p[task % 2]
                if task == 0:
                    pe.wait_ge(xn_ok, NB * (q + 1))
                    if not first:
                        pe.wait_ge(krows_ok, G * q)
                    for b in range(NB):
                        mm = pe.transpose(bank[:, b * S:(b + 1) * S], xn[:, b, :], ident[:])
                    mm.then_inc(xt_ps, 1)
                elif task == 1:
                    pe.wait_ge(fill_ok, NB * (q + 1) + 1)
                    pe.wait_ge(ld_ctx[par], 16 * (k + 1))
                    for b in range(NB):
                        mm = pe.matmul(bank[:, b * KV:(b + 1) * KV], context_in[:, par, b, :], fill[:, b, :],
                                       start=True, stop=True)
                    mm.then_inc(ct_ps, 1)
                elif task == 2:
                    pe.wait_ge(xt_ok, q + 1)
                    pe.matmul(bank[:], w_t[:, 0, :], xn_t[:], start=True, stop=True).then_inc(q_ps, 1)
                elif task == 3:
                    pe.wait_ge(ct_ok, q + 1)
                    pe.matmul(bank[:, 0:NB * KV], w_t[:, 1, :], context_t[:].rearrange("p b k -> p (b k)"),
                              start=True, stop=True).then_inc(k_ps, 1)
                elif task < 8:
                    g = task - 4
                    if g == 0:
                        pe.wait_ge(sel_ok, 1)
                        pe.wait_ge(qhi_ok, q + 1)
                        pe.wait_ge(qlo_ok, q + 1)
                    elif g == 1:
                        pe.wait_ge(klo_ok, q + 1)
                    else:
                        pe.wait_ge(qrows_ok, G * q + g - 1)
                    pe.matmul(bank[:], select["q_hi_sel"][:, g, :], q_hi[:], start=True, stop=False)
                    pe.matmul(bank[:], select["q_lo_sel"][:, g, :], q_lo[:], start=False, stop=True) \
                        .then_inc(qrows_ps, 1)
                elif task == 8:
                    pe.wait_ge(qrows_ok, G * q + 3)
                    for b in range(NB):
                        mm = pe.matmul(bank[0:KV, b * D:(b + 1) * D], context_t[:, b, :], w_t[:, 2, :],
                                       start=True, stop=True)
                    mm.then_inc(v_ps, 1)
                else:
                    g = task - 9
                    if g == 0:
                        pe.wait_ge(khi_ok, q + 1)
                        pe.wait_ge(klo_ok, q + 1)
                        pe.wait_ge(qrows_ok, G * (q + 1))
                    elif g == 1:
                        pe.wait_ge(v_ok, (2 * NB + 2) * (q + 1))
                    else:
                        pe.wait_ge(krows_ok, G * q + g - 1)
                    pe.matmul(bank[:, 0:NB * KV], select["k_hi_sel"][:, g, :], k_hi[:], start=True, stop=False)
                    pe.matmul(bank[:, 0:NB * KV], select["k_lo_sel"][:, g, :], k_lo[:], start=False, stop=True) \
                        .then_inc(krows_ps, 1)

            def scores(t, b, par, g, first=False):
                if g >= 2 or not first:
                    pe.wait_ge(max_ok, G * t + g - 1)
                for j in range(J):
                    mm = pe.matmul(ps_s[g % 2][:, j * KV:(j + 1) * KV], q_slots[par][:, g, j, b, :],
                                   k_rows[par][:, g, b, :], start=True, stop=True)
                mm.then_inc(s_ps, 1)

            def shifted(t, b, par, g):
                pe.wait_ge(exp_ok, EXP0 + G * t + g - 1)
                pe.wait_ge(max_ok, G * t + g + 1)
                bank = ps_st[g % 2][0:KV, :]
                pe.matmul(bank, k_rows[par][:, g, b, :], q_slots[par][:, g, :, b, :], start=True, stop=False)
                for j in range(J):
                    mm = pe.matmul(bank[:, j * S:(j + 1) * S],
                                   neg_max[:, b % 2, J * g + j:J * g + j + 1].to_broadcast([S, KV]),
                                   ident_r[:], start=False, stop=(j == J - 1))
                mm.then_inc(st_ps, 1)

            def products(t, q, b, par, g):
                pe.wait_ge(exp_ok, EXP0 + G * t + g + 1)
                if g == 0:
                    pe.wait_ge(o_ok, O0 + t)
                    if b == 0:
                        pe.wait_ge(v_ok, (2 * NB + 2) * (q + 1))
                half_of = slice(0, S) if g < 3 else slice(S, 2 * S)
                for j in range(J):
                    mm = pe.matmul(ps_o[32 * j:32 * j + 32, half_of], v_blocks[par][:, b, J * g + j, :],
                                   probs[:, g, j, :], start=(g in (0, 3)), stop=(g in (2, 3)))
                if g == 3:
                    mm.then_inc(o_ps, 1)

            def turn_back(t):
                pe.wait_ge(o_ok, O0 + t)
                pe.wait_ge(x2_ok, X20 + t)
                for n in range(2):
                    mm = pe.transpose(ps_t[:, n * S:(n + 1) * S], att_t[:, n, :], ident[:])
                mm.then_inc(t_ps, 1)

            for task in range(NT):
                prepare(task, 0, 0, first=True)
            pe.wait_ge(krows_ok, G)
            pe.wait_ge(qslots_ok, 16 * J)
            for g in range(G):
                scores(0, 0, 0, g, first=True)
            pe.wait_ge(ident_r_ok, 1)
            pe.wait_ge(share_ok, 1)

            def step(k, par, ahead):
                q = 2 * k + par
                for b in range(NB):
                    t = NB * q + b
                    for g in range(G):
                        shifted(t, b, par, g)
                        if g:
                            products(t, q, b, par, g - 1)
                        if g == 1:
                            turn_back(t)
                        if b < 3:
                            scores(t + 1, b + 1, par, g)
                        elif ahead:
                            if g == 0:
                                pe.wait_ge(krows_ok, G * (q + 2))
                                pe.wait_ge(qslots_ok, 16 * J * (q + 2))
                            scores(t + 1, 0, 1 - par, g)
                        if ahead and b < 3:
                            prepare(G * b + g, k + par, 1 - par)
                    if ahead and b == 2:
                        prepare(NT - 1, k + par, 1 - par)
                    products(t, q, b, par, 3)

            quads(pe, step)
            turn_back(B)

            pe.wait_ge(abs_ok, 2)
            pe.matmul(ps_o[:, 0:2], ones[:], abs_sum[:], start=True, stop=True).then_inc(abs_ps, 1)
            for c in range(2 * FC):
                if c == 0:
                    pe.wait_ge(tern_ok, 2)
                if c >= 2:
                    pe.wait_ge(ternt_ok, c - 1)
                pe.transpose(ps_s[c % 2][:, 0:128], tern[:, c // FC, (c % FC) * 128:(c % FC + 1) * 128], ident[:]) \
                    .then_inc(ternt_ps, 1)

            def turn_y(q):
                pe.wait_ge(y_ok, NB * (q + 1))
                for b in range(NB):
                    mm = pe.transpose(ps_p[0][:, b * S:(b + 1) * S], y[:, b, :], ident[:])
                mm.then_inc(yt_ps, 1)

            def up(q, par):
                pe.wait_ge(yt_ok, q + 1)
                for c in range(FC):
                    pe.wait_ge(gelu_ok, FC * q + c + 1)
                    pe.matmul(up_banks[c][:], wu_t[:, c * 128:(c + 1) * 128], y_t[:], start=True, stop=True) \
                        .then_inc(up_ps, 1)

            def down(q, par):
                pe.wait_ge(res_ok, NB * q + 1)
                for b in range(NB):
                    for c in range(FC):
                        if b == 0:
                            pe.wait_ge(gelu_ok, GELU0 + FC * q + c + 1)
                        mm = pe.matmul(ps_t[:, b * D:(b + 1) * D], act_h[par][:, c, b * S:(b + 1) * S], wd_t[:, c, :],
                                       start=(c == 0), stop=(c == FC - 1))
                mm.then_inc(down_ps, 1)
                pe.wait_ge(sqsum_ok, q + 2)
                for b in range(NB):
                    mm = pe.matmul(ps_o[:, b:b + 1], square_sum[:, b * S:(b + 1) * S], ones[:, 0:1],
                                   start=True, stop=True)
                mm.then_inc(ssq_ps, 1)

            pe.wait_ge(ternt_ok, 2 * FC)
            turn_y(0)

            with pe.Fori(0, QUADS // 2 - 1) as it:
                for par in range(2):
                    up(2 * it + par, par)
                    turn_y(2 * it + par + 1)
                    down(2 * it + par, par)
            up(QUADS - 2, 0)
            turn_y(QUADS - 1)
            down(QUADS - 2, 0)
            up(QUADS - 1, 1)
            down(QUADS - 1, 1)

        @block.vector
        def _(dve):
            dve.wait_ge(ld_small, 16 * 6)
            dve.tensor_copy(mask_rows_f[:], mask_rows[:]).then_inc(maskf_ok, 1)
            for n in select:
                dve.memset(select[n][:].bitcast(F32), 0.0).then_inc(sel_zero, 1)
            dve.wait_ge(sel_zero, 4)
            dve.wait_ge(ident_ok, 1)
            dve.tensor_copy(ident_r[:], ident[:]).then_inc(ident_r_ok, 1)
            parts = {"q_hi_sel": (0, 1), "q_lo_sel": (2, 3), "k_hi_sel": (0, 2), "k_lo_sel": (1, 3)}
            for n, cs in parts.items():
                for c in cs:
                    last = dve.tensor_copy(
                        select[n][:].rearrange("p g (j c i) -> p g j c i", j=J, c=C)[:, :, :, c, :],
                        ident[:].rearrange("p (g j i) -> p g j i", g=G, j=J))
            last.then_inc(sel_ok, 1)
            dve.wait_ge(tanh_ok, 1)
            dve.tensor_scalar(gated_bias[:], v_bias[:], tanh_g[:, 0:1], None, ALU.mult).then_inc(gbias_ok, 1)
            dve.wait_ge(maskt_ps, 1)
            dve.tensor_scalar(valid[:], ps_o[0:KV, 0:B], 0.0, None, ALU.not_equal).then_inc(valid_ok, 1)
            dve.wait_ge(count_ps, 1)
            dve.tensor_scalar(valid_n[:], ps_t[0:KV, 0:B], 1.0, None, ALU.max).then_inc(count_ok, 1)
            dve.wait_ge(count_ok, 1)
            dve.reciprocal(valid_share[:], valid_n[:]).then_inc(count_ok, 1)
            dve.wait_ge(count_ok, 2)
            dve.wait_ge(valid_ok, 1)
            dve.tensor_tensor(valid_share[:], valid_share[:], valid[:], ALU.mult).then_inc(share_ok, 1)
            dve.wait_ge(share_ok, 1)
            dve.memset(var2[:], 0.0).then_inc(fill_ok, 1)

            def ahead_of(k, par):
                q = 2 * k + par
                dve.wait_ge(ld_x[par], 16 * (k + 1))
                dve.wait_ge(ld_mask, 16 * (q + 1))
                dve.tensor_scalar(invalid[:].rearrange("p b k -> p (b k)"), mask_in[:], 0.0, None, ALU.is_equal) \
                    .then_inc(invalid_ok, 1)
                for b in range(NB):
                    dve.bn_stats(stats[:, b, :], xs[:, q * NB + b + 1, :]).then_inc(stats_ok, 1)
                dve.wait_ge(invalid_ok, q + 1)
                dve.wait_ge(stats_ok, NB * (q + 1))
                for b in range(NB):
                    dve.wait_ge(diag_ok, NB * q + b + 1)
                    dve.scalar_tensor_tensor(out=fill[:, b, :], in0=invalid[:, b, :],
                                             scalar=valid_share[:, bass.ds(q * NB + b, 1)], in1=diag[:, b, :],
                                             op0=ALU.mult, op1=ALU.add).then_inc(fill_ok, 1)
                for b in range(NB):
                    dve.bn_aggr(moments[:, b, :], stats[:, b, :]).then_inc(moments_ok, 1)
                dve.wait_ge(moments_ok, NB * (q + 1))
                dve.tensor_scalar(var_eps[:], moments[:, :, 1], LN_EPS, None, ALU.add).then_inc(vareps_ok, 1)
                dve.wait_ge(rstd_ok, q + 1)
                for b in range(NB):
                    dve.tensor_scalar(xn[:, b, :], xs[:, q * NB + b + 1, :], moments[:, b, 0:1], rstd[:, b:b + 1],
                                      ALU.subtract, ALU.mult).then_inc(xn_ok, 1)

            def evacuate(task, q, par):
                bank = ps_p[task % 2]
                if task == 1:
                    dve.wait_ge(ct_ps, q + 1)
                    dve.tensor_copy(context_t[:].rearrange("p b k -> p (b k)"), bank[:, 0:NB * KV]) \
                        .then_inc(ct_ok, 1)
                elif task == 2:
                    dve.wait_ge(qhi_ok, q + 1)
                    dve.scalar_tensor_tensor(out=q_lo[:], in0=bank[:], scalar=q_bias[:, 0:1],
                                             in1=q_hi[:].bitcast(F32), op0=ALU.add, op1=ALU.subtract) \
                        .then_inc(qlo_ok, 1)
                elif task == 3:
                    dve.wait_ge(khi_ok, q + 1)
                    dve.scalar_tensor_tensor(out=k_lo[:], in0=bank[:, 0:NB * KV], scalar=k_bias[:, 0:1],
                                             in1=k_hi[:].bitcast(F32), op0=ALU.add, op1=ALU.subtract) \
                        .then_inc(klo_ok, 1)
                elif task == 8:
                    dve.wait_ge(v_ps, q + 1)
                    base = NB * H * VC
                    for b in range(NB):
                        keep = valid[:, bass.ds(q * NB + b, 1)]
                        dve.tensor_scalar(bass.AP(v_store[par], b * H * VC,
                                                  [[base, KV], [J * VC + HD, 3], [VC, J], [1, HD]]),
                                          bank[0:KV, b * D:b * D + 96].rearrange("p (a j i) -> p a j i", a=3, j=J),
                                          keep, tanh_g[0:KV, 0:1], ALU.mult, ALU.mult).then_inc(v_ok, 1)
                        dve.tensor_scalar(v_blocks[par][:, b, 12:16, 0:HD],
                                          bank[0:KV, b * D + 96:(b + 1) * D].rearrange("p (j i) -> p j i", j=J),
                                          keep, tanh_g[0:KV, 0:1], ALU.mult, ALU.mult).then_inc(v_ok, 1)
                    keep = valid[:, bass.ds(q * NB, NB)]
                    dve.tensor_copy(bass.AP(v_store[par], 24, [[base, KV], [H * VC, NB], [J * VC + 1, 3], [VC, J]]),
                                    keep.rearrange("p (b o n) -> p b o n", o=1, n=1).to_broadcast([KV, NB, 3, J])) \
                        .then_inc(v_ok, 1)
                    dve.tensor_copy(v_blocks[par][:, :, 12:16, 24],
                                    keep.rearrange("p (b o) -> p b o", o=1).to_broadcast([KV, NB, J])) \
                        .then_inc(v_ok, 1)
                elif task > 8:
                    g = task - 9
                    dve.wait_ge(krows_ps, G * q + g + 1)
                    dve.tensor_copy(k_rows[par][:, g].rearrange("p b k -> p (b k)"), bank[:, 0:NB * KV]) \
                        .then_inc(krows_ok, 1)

            def maximum(t, b, g):
                dve.wait_ge(s_ps, G * t + g + 1)
                dve.tensor_reduce(neg_max[:, b % 2, J * g:J * g + J],
                                  ps_s[g % 2][:, 0:J * KV].rearrange("p (j k) -> p j k", j=J),
                                  AX.X, ALU.max, negate=True).then_inc(max_ok, 1)

            def finish(t):
                tb = ps_t[:]
                dve.wait_ge(t_ps, t + 1)
                first = tb[:, 0:128].rearrange("p (j c) -> p j c", j=J)
                second = tb[:, 128:256].rearrange("p (j c) -> p j c", j=J)
                dve.reciprocal(inv_den[:, 0:12].rearrange("p (a j) -> p a j", a=3),
                               first[:, :, 24:27].rearrange("p j a -> p a j")).then_inc(den_ok, 1)
                dve.reciprocal(inv_den[:, 12:16], second[:, :, 24]).then_inc(den_ok, 1)
                dve.wait_ge(den_ok, 2 * t + 1)
                dve.tensor_tensor(att[:, 0:96].rearrange("p (a j i) -> p a j i", a=3, j=J),
                                  first[:, :, 0:24].rearrange("p j (a i) -> p a j i", a=3),
                                  inv_den[:, 0:12].rearrange("p (a j o) -> p a j o", a=3, o=1)
                                  .to_broadcast([S, 3, J, HD]), ALU.mult).then_inc(att_ok, 1)
                dve.wait_ge(den_ok, 2 * t + 2)
                dve.tensor_tensor(att[:, 96:128].rearrange("p (j i) -> p j i", j=J), second[:, :, 0:HD],
                                  inv_den[:, 12:16].rearrange("p (j o) -> p j o", o=1).to_broadcast([S, J, HD]),
                                  ALU.mult).then_inc(att_ok, 1)
                dve.wait_ge(att_ok, 2 * t + 2)
                dve.tensor_tensor(xs[:, t, :], xs[:, t, :], att[:], ALU.add).then_inc(x2_ok, 1)

            def measure(t):
                dve.bn_stats(stats2[:, t], xs[:, t, :]).then_inc(stats2_ok, 1)

            ahead_of(0, 0)
            for task in range(8):
                evacuate(task, 0, 0)
            dve.wait_ge(const_ok, 5)
            for task in range(8, NT):
                evacuate(task, 0, 0)
            for g in range(G):
                maximum(0, 0, g)
            dve.memset(xs[:, 0, :], 0.0).then_inc(x2_ok, X20)
            dve.memset(inv_den[:], 0.0).then_inc(exp_ok, EXP0)
            ahead_of(0, 1)
            dve.wait_ge(x2_ok, X20)

            def step(k, par, ahead):
                q = 2 * k + par
                for b in range(NB):
                    t = NB * q + b
                    for g in range(G):
                        if g == 2:
                            dve.wait_ge(x2_ok, X20 + t + 1)
                        if b < 3 or ahead:
                            maximum(t + 1, b + 1, g)
                        if g == 2:
                            measure(t)
                        if ahead and b < 3:
                            evacuate(G * b + g, q + 1, 1 - par)
                        if g == 1:
                            if b == 1:
                                dve.wait_ge(xb_ok, q + 1)
                            finish(t)
                    if ahead and b == 2:
                        evacuate(NT - 1, q + 1, 1 - par)
                if ahead == 2:
                    dve.wait_ge(xt_ps, q + 2)
                    dve.wait_ge(ct_ps, q + 2)
                    ahead_of(k + 1, par)

            quads(dve, step)
            finish(B)
            dve.wait_ge(x2_ok, X20 + B + 1)
            measure(B)
            dve.wait_ge(stats2_ok, B + 1)
            even, odd = stats2[:, :, 0], stats2[:, :, 1]
            dve.tensor_tensor(mean2[:], even[:, :, 1], odd[:, :, 1], ALU.add).then_inc(moments2_ok, 1)
            dve.tensor_tensor(mean_gap[:], even[:, :, 1], odd[:, :, 1], ALU.subtract).then_inc(moments2_ok, 1)
            dve.tensor_tensor(var2[:], even[:, :, 2], odd[:, :, 2], ALU.add).then_inc(moments2_ok, 1)
            dve.wait_ge(moments2_ok, 3)
            dve.tensor_scalar(mean2[:], mean2[:], 0.5, None, ALU.mult).then_inc(gap_ok, 1)
            dve.scalar_tensor_tensor(out=mean_gap[:], in0=mean_gap[:], scalar=0.25, in1=mean_gap[:],
                                     op0=ALU.mult, op1=ALU.mult).then_inc(gap_ok, 1)
            dve.wait_ge(gap_ok, 2)
            dve.scalar_tensor_tensor(out=var2[:], in0=var2[:], scalar=1.0 / D, in1=mean_gap[:],
                                     op0=ALU.mult, op1=ALU.add).then_inc(moments2_ok, 1)
            dve.wait_ge(moments2_ok, 4)
            dve.tensor_scalar(var2_eps[:], var2[:], LN_EPS, None, ALU.add).then_inc(moments2_ok, 1)

            dve.wait_ge(ld_ffn, 32)
            raws = [wu_raw[:].rearrange("p c d -> p (c d)"), wd_raw[:]]
            for n in range(2):
                dve.tensor_reduce(abs_sum[:, n:n + 1], raws[n], AX.X, ALU.add, apply_absolute_value=True) \
                    .then_inc(abs_ok, 1)
            dve.wait_ge(abs_ps, 1)
            dve.tensor_scalar(thresh[:], ps_o[:, 0:2], 1.0 / (F * D), 0.5, ALU.mult, ALU.mult).then_inc(thresh_ok, 1)
            dve.tensor_scalar(neg_thresh[:], ps_o[:, 0:2], 1.0 / (F * D), -0.5, ALU.mult, ALU.mult) \
                .then_inc(thresh_ok, 1)
            dve.wait_ge(thresh_ok, 2)
            for n in range(2):
                dve.tensor_scalar(tern_neg[:, n, :], raws[n], neg_thresh[:, n:n + 1], None, ALU.is_lt).then_inc(neg_ok, 1)
            for n in range(2):
                dve.wait_ge(neg_ok, n + 1)
                dve.scalar_tensor_tensor(out=tern[:, n, :], in0=raws[n], scalar=thresh[:, n:n + 1],
                                         in1=tern_neg[:, n, :], op0=ALU.is_gt, op1=ALU.subtract) \
                    .then_inc(tern_ok, 1)
            dve.wait_ge(root_ok, 2)
            dve.scalar_tensor_tensor(out=ffn_den[:], in0=root_eps[:], scalar=RMS_EPS, in1=root[:],
                                     op0=ALU.mult, op1=ALU.add).then_inc(den2_ok, 1)
            dve.wait_ge(den2_ok, 1)
            dve.reciprocal(ffn_scale[:], ffn_den[:]).then_inc(scale2_ok, 1)
            dve.wait_ge(scale2_ok, 1)
            dve.memset(square_sum[:], 0.0).then_inc(sqsum_ok, 1)
            dve.memset(rms_inv[:], 0.0).then_inc(res_ok, 1)
            dve.memset(out_scale[:], 0.0).then_inc(gelu_ok, GELU0)

            def norm(q):
                for b in range(NB):
                    dve.tensor_scalar(y[:, b, :], xs[:, q * NB + b + 1, :],
                                      mean2[:, bass.ds(q * NB + b + 1, 1)], ffn_scale[:, bass.ds(q * NB + b + 1, 1)],
                                      ALU.subtract, ALU.mult).then_inc(y_ok, 1)

            def ffn(q, par, more):
                if more:
                    dve.wait_ge(yt_ps, q + 1)
                    norm(q + 1)
                dve.wait_ge(sq_ok, FC * (q + 1))
                dve.tensor_reduce(square_sum[:], squares[:].rearrange("p c n -> p n c"), AX.X, ALU.add) \
                    .then_inc(sqsum_ok, 1)
                dve.wait_ge(ssq_ps, q + 1)
                dve.tensor_scalar(mean_sq[:], ps_o[:, 0:NB], 1.0 / F, None, ALU.mult).then_inc(meansq_ok, 1)
                dve.wait_ge(rms_ok, q + 1)
                dve.tensor_scalar(rms_inv[:], rms[:], RMS_EPS, None, ALU.add).then_inc(rmse_ok, 1)
                dve.wait_ge(rmse_ok, q + 1)
                dve.reciprocal(rms_inv[:], rms_inv[:]).then_inc(rinv_ok, 1)
                dve.wait_ge(rinv_ok, q + 1)
                dve.tensor_scalar(out_scale[:], rms_inv[:], tanh_g[:, 1:2], None, ALU.mult).then_inc(oscale_ok, 1)
                dve.wait_ge(oscale_ok, q + 1)
                dve.wait_ge(down_ps, q + 1)
                for b in range(NB):
                    dve.scalar_tensor_tensor(out=xs[:, q * NB + b + 1, :], in0=ps_t[:, b * D:(b + 1) * D],
                                             scalar=out_scale[:, b:b + 1], in1=xs[:, q * NB + b + 1, :],
                                             op0=ALU.mult, op1=ALU.add).then_inc(res_ok, 1)

            norm(0)
            with dve.Fori(0, QUADS // 2 - 1) as it:
                for par in range(2):
                    ffn(2 * it + par, par, True)
            ffn(QUADS - 2, 0, True)
            ffn(QUADS - 1, 1, False)


_INS = ["x", "ctx_1024", "mask_Bx1x1xS2_ik0", "g_xattn", "g_ffn", "L0_xattn_Wq", "L0_xattn_bq", "L0_xattn_Wk",
        "L0_xattn_bk", "L0_xattn_Wv", "L0_xattn_bv", "L0_ffn_w_up", "L0_ffn_w_down"]


def kernel(**inputs):
    import numpy as np
    import concourse.bacc as bacc
    from concourse.bass_utils import run_bass_kernel_spmd

    nc = bacc.Bacc("TRN2", target_bir_lowering=False, num_devices=1)
    arrays, args = {}, []
    for name in _INS:
        a = np.ascontiguousarray(inputs[name])
        if name.startswith("mask"):
            a = a.reshape(B, KV)
        arrays[f"in_{name}"] = a
        args.append(nc.dram_tensor(f"in_{name}", a.shape, mybir.dt.from_np(a.dtype), kind="ExternalInput").ap())
    out = nc.dram_tensor("out_0", (B, S, D), F32, kind="ExternalOutput").ap()
    flamingo_kernel(nc, *args, out)
    r = run_bass_kernel_spmd(nc, [arrays], core_ids=[0])
    return r.results[0]["out_0"]
```

```python
from contextlib import ExitStack

import concourse.bass as bass
from concourse import mybir

F32 = mybir.dt.float32
F32R = mybir.dt.float32r
BF16 = mybir.dt.bfloat16
I32 = mybir.dt.int32
ALU = mybir.AluOpType
ACT = mybir.ActivationFunctionType
AX = mybir.AxisListType

B, S, D = 32, 128, 128
KV = 120
H, HD = 16, 8
F = 512
NB = 4
QUADS = B // NB
G, J = 4, 4
C = 4
FC = F // 128
FS = 3
LN_EPS = 1e-5
RMS_EPS = 1e-8
SCALE = float(HD) ** -0.5
VC = 32
NT = 3 * G + 1


def flamingo_kernel(nc, x, context, mask, g_xattn, g_ffn, wq, bq, wk, bk, wv, bv, w_up, w_down, out):
    ctx = ExitStack()
    with ctx:
        def sb(name, shape, dt=F32):
            return ctx.enter_context(nc.sbuf_tensor(name, shape, dt))

        def psum(name, shape):
            return ctx.enter_context(nc.psum_tensor(name, shape, F32))

        def sem(name):
            return ctx.enter_context(nc.semaphore(name))

        xs = sb("xs", [S, B + 1, D])
        ident = sb("ident", [128, 128])
        ident_b = sb("ident_b", [128, 128], BF16)
        ones = sb("ones", [128, 128])
        select = {n: sb(n, [128, G, 128], F32R) for n in ("q_hi_sel", "q_lo_sel", "k_hi_sel", "k_lo_sel")}
        w_raw = sb("w_raw", [128, 3, D])
        w_t = sb("w_t", [128, 3, D])
        q_bias = sb("q_bias", [128, 1])
        k_bias = sb("k_bias", [128, 1])
        v_bias = sb("v_bias", [128, D])
        gates = sb("gates", [128, 2])
        tanh_g = sb("tanh_g", [128, 2])
        gated_bias = sb("gated_bias", [128, D])
        mask_rows = sb("mask_rows", [B, KV], I32)
        mask_rows_f = sb("mask_rows_f", [B, KV])
        valid = sb("valid", [KV, B])
        valid_n = sb("valid_n", [KV, B])
        valid_share = sb("valid_share", [KV, B])
        minus_half = sb("minus_half", [128, B + 1])
        half = sb("half", [128, B + 1])

        context_in = sb("context_in", [KV, 2, NB, D])
        mask_in = sb("mask_in", [KV, NB * KV], I32)
        invalid = sb("invalid", [KV, NB, KV])
        diag = sb("diag", [KV, NB, KV])
        fill = sb("fill", [KV, NB, KV])
        stats = sb("stats", [S, NB, 6])
        moments = sb("moments", [S, NB, 2])
        var_eps = sb("var_eps", [S, NB])
        rstd = sb("rstd", [S, NB])
        xn = sb("xn", [S, NB, D])
        xn_t = sb("xn_t", [D, NB * S])
        context_t = sb("context_t", [D, NB, KV])
        q_hi = sb("q_hi", [128, NB * S], F32R)
        q_lo = sb("q_lo", [128, NB * S], F32R)
        k_hi = sb("k_hi", [128, NB * KV], F32R)
        k_lo = sb("k_lo", [128, NB * KV], F32R)
        q_rows = [sb(f"q_rows{p}", [128, G, NB * S], F32R) for p in range(2)]
        k_rows = [sb(f"k_rows{p}", [128, G, NB, KV], F32R) for p in range(2)]
        q_slots = [sb(f"q_slots{p}", [128, G, J, NB // 2, S], F32R) for p in range(2)]
        k_slots = [sb(f"k_slots{p}", [128, G, J, NB // 2, KV], F32R) for p in range(2)]
        v_store = [sb(f"v_blocks{p}", [128, NB, H, VC]) for p in range(2)]
        v_blocks = [v[0:KV] for v in v_store]
        neg_max = sb("neg_max", [S, 2, H], BF16)
        p_store = sb("probs", [128, G, J, S])
        probs = p_store[0:KV]
        att_t = sb("att_t", [128, 2, S])
        inv_den = sb("inv_den", [S, H])
        att = sb("att", [S, D])
        stats2 = sb("stats2", [S, B + 1, 2, 3])
        mean2 = sb("mean2", [S, B + 1])
        mean_gap = sb("mean_gap", [S, B + 1])
        var2 = sb("var2", [S, B + 1])
        root = sb("root", [S, B + 1])
        var2_eps = sb("var2_eps", [S, B + 1])
        root_eps = sb("root_eps", [S, B + 1])
        ffn_den = sb("ffn_den", [S, B + 1])
        ffn_scale = sb("ffn_scale", [S, B + 1])

        wu_raw = sb("wu_raw", [128, FC, D])
        wd_raw = sb("wd_raw", [D, F])
        tern = sb("tern", [128, 2, F])
        tern_neg = sb("tern_neg", [128, 2, F])
        abs_sum = sb("abs_sum", [128, 2])
        thresh = sb("thresh", [128, 2])
        neg_thresh = sb("neg_thresh", [128, 2])
        wu_t = sb("wu_t", [D, F], F32R)
        wd_t = sb("wd_t", [128, FC, D], F32R)
        y = sb("y", [S, NB, D])
        y_hi, y_lo = q_hi, q_lo
        act_h = [v[:].rearrange("p b h c -> p (b h c)").rearrange("p (c n) -> p c n", c=FC) for v in v_store]
        squares = p_store[:].rearrange("p g j s -> p g (j s)")
        h_hi = [r[:, 0:FS, :] for r in q_rows]
        h_lo = [k[:].rearrange("p g j b k -> p (g j b k)")[:, 0:FS * NB * S].rearrange("p (c n) -> p c n", c=FS)
                for k in k_slots]
        ffn_t = sb("ffn_t", [D, NB * S])
        square_sum = sb("square_sum", [128, 2, NB * S])
        pair_sum = sb("pair_sum", [128, 2, NB * S])
        gelu_warm = sb("gelu_warm", [128, 1])
        mean_sq = sb("mean_sq", [S, NB])
        rms = sb("rms", [S, NB])
        rms_inv = sb("rms_inv", [S, NB])
        out_scale = sb("out_scale", [S, NB])

        ps_s = [psum(f"ps_s{i}", [128, 512]) for i in range(2)]
        ps_st = [psum(f"ps_st{i}", [128, 512]) for i in range(2)]
        ps_o = psum("ps_o", [128, 512])
        ps_t = psum("ps_t", [128, 512])
        ps_p = [psum(f"ps_p{i}", [128, 512]) for i in range(2)]

        ld_x = [sem(f"ld_x{p}") for p in range(2)]
        ld_w = sem("ld_w")
        ld_masks = sem("ld_masks")
        ld_gates = sem("ld_gates")
        ld_bias = sem("ld_bias")
        ld_ctx = [sem(f"ld_ctx{p}") for p in range(2)]
        ld_mask = sem("ld_mask")
        ld_ffn = sem("ld_ffn")
        ident_zero = sem("ident_zero")
        ident_ok = sem("ident_ok")
        ident_b_ok = sem("ident_b_ok")
        ones_ok = sem("ones_ok")
        power_ok = sem("power_ok")
        vzero_ok = sem("vzero_ok")
        sel_zero = sem("sel_zero")
        sel_ok = sem("sel_ok")
        pad_ok = sem("pad_ok")
        tanh_ok = sem("tanh_ok")
        gbias_ok = sem("gbias_ok")
        wt_ps = sem("wt_ps")
        wt_ok = sem("wt_ok")
        maskf_ok = sem("maskf_ok")
        maskt_ps = sem("maskt_ps")
        valid_ok = sem("valid_ok")
        count_ps = sem("count_ps")
        count_ok = sem("count_ok")
        share_ok = sem("share_ok")
        stats_ok = sem("stats_ok")
        moments_ok = sem("moments_ok")
        vareps_ok = sem("vareps_ok")
        rstd_ok = sem("rstd_ok")
        xn_ok = sem("xn_ok")
        xb_ok = sem("xb_ok")
        invalid_ok = sem("invalid_ok")
        diag_ok = sem("diag_ok")
        fill_ok = sem("fill_ok")
        xt_ps = sem("xt_ps")
        xt_ok = sem("xt_ok")
        ct_ps = sem("ct_ps")
        ct_ok = sem("ct_ok")
        q_ps = sem("q_ps")
        qhi_ok = sem("qhi_ok")
        qlo_ok = sem("qlo_ok")
        k_ps = sem("k_ps")
        khi_ok = sem("khi_ok")
        klo_ok = sem("klo_ok")
        v_ps = sem("v_ps")
        v_ok = sem("v_ok")
        qrows_ps = sem("qrows_ps")
        qrows_ok = sem("qrows_ok")
        qslots_ok = [sem(f"qslots_ok{p}") for p in range(2)]
        kslots_ok = [sem(f"kslots_ok{p}") for p in range(2)]
        krows_ps = sem("krows_ps")
        krows_ok = sem("krows_ok")
        s_ps = sem("s_ps")
        max_ok = sem("max_ok")
        st_ps = sem("st_ps")
        exp_ok = sem("exp_ok")
        o_ps = sem("o_ps")
        o_ok = sem("o_ok")
        t_ps = sem("t_ps")
        den_ok = sem("den_ok")
        att_ok = sem("att_ok")
        x2_ok = sem("x2_ok")
        stats2_ok = sem("stats2_ok")
        moments2_ok = sem("moments2_ok")
        gap_ok = sem("gap_ok")
        root_ok = sem("root_ok")
        den2_ok = sem("den2_ok")
        scale2_ok = sem("scale2_ok")
        abs_ok = sem("abs_ok")
        abs_ps = sem("abs_ps")
        thresh_ok = sem("thresh_ok")
        neg_ok = sem("neg_ok")
        tern_ok = sem("tern_ok")
        ternt_ps = sem("ternt_ps")
        ternt_ok = sem("ternt_ok")
        y_ok = sem("y_ok")
        yt_ps = sem("yt_ps")
        yhi_ok = sem("yhi_ok")
        ylo_ok = sem("ylo_ok")
        hhi_ok = sem("hhi_ok")
        hlo_ok = sem("hlo_ok")
        ft_ok = sem("ft_ok")
        back_ps = sem("back_ps")
        up_ps = sem("up_ps")
        gelu_ok = sem("gelu_ok")
        sq_ok = sem("sq_ok")
        sqsum_ok = sem("sqsum_ok")
        down_ps = sem("down_ps")
        ssq_ps = sem("ssq_ps")
        meansq_ok = sem("meansq_ok")
        rms_ok = sem("rms_ok")
        rmse_ok = sem("rmse_ok")
        pairs_ok = sem("pairs_ok")
        rinv_ok = sem("rinv_ok")
        oscale_ok = sem("oscale_ok")
        res_ok = sem("res_ok")
        st_out = sem("st_out")

        EXP0, O0, X20 = 2, 1, 1
        GELU0, SUM0, MEANSQ0, FT0, RES0 = FC, 1, 1, 1, 1

        up_banks = ps_s + ps_st

        SEGMENTS = (slice(0, B + 1 - 2 * NB), slice(B + 1 - 2 * NB, B + 1 - NB), slice(B + 1 - NB, B + 1))

        block = ctx.enter_context(nc.Block())

        def quads(eng, step):
            with eng.Fori(0, QUADS // 2 - 1) as it:
                for par in range(2):
                    step(it, par, 2)
            step(QUADS // 2 - 1, 0, 1)
            step(QUADS // 2 - 1, 1, 0)

        def quads_deep(eng, step):
            with eng.Fori(0, QUADS // 2 - 2) as it:
                for par in range(2):
                    step(it, par, 3)
            for last in range(4):
                step(QUADS // 2 - 2 + last // 2, last % 2, 3 - last)

        @block.sync
        def _(sp):
            def load_x(q, par):
                sp.dma_start(xs[:, bass.ds(q * NB + 1, NB), :], x[bass.ds(q * NB, NB)].rearrange("b s d -> s b d")) \
                    .then_inc(ld_x[par], 16)

            sp.dma_start(mask_rows[:], mask).then_inc(ld_masks, 16)
            load_x(0, 0)
            sp.dma_start(context_in[:, 0], context[0:NB].rearrange("b k d -> k b d")).then_inc(ld_ctx[0], 16)
            sp.dma_start(mask_in[:], mask[0:NB].rearrange("b k -> (b k)").rearrange("(o n) -> o n", o=1)
                         .to_broadcast([KV, NB * KV])).then_inc(ld_mask, 16)
            for n, w in enumerate((wq, wk, wv)):
                sp.dma_start(w_raw[:, n, :], w).then_inc(ld_w, 16)
            for n, g in enumerate((g_xattn, g_ffn)):
                sp.dma_start(gates[:, n:n + 1], g.rearrange("(o n) -> o n", o=1).to_broadcast([128, 1])) \
                    .then_inc(ld_gates, 16)

            def load_context(q, par):
                sp.dma_start(context_in[:, par], context[bass.ds(q * NB, NB)].rearrange("b k d -> k b d")) \
                    .then_inc(ld_ctx[par], 16)

            def load_mask(q):
                sp.dma_start(mask_in[:], mask[bass.ds(q * NB, NB)].rearrange("b k -> (b k)")
                             .rearrange("(o n) -> o n", o=1).to_broadcast([KV, NB * KV])).then_inc(ld_mask, 16)

            sp.dma_start(q_bias[:], bq.rearrange("(p o) -> p o", o=1)).then_inc(ld_bias, 16)
            sp.dma_start(k_bias[:], bk.rearrange("(p o) -> p o", o=1)).then_inc(ld_bias, 16)
            sp.dma_start(v_bias[:], bv.rearrange("(o n) -> o n", o=1).to_broadcast([128, D])).then_inc(ld_bias, 16)
            sp.dma_start(wu_raw[:], w_up.rearrange("(c p) d -> p c d", p=128)).then_inc(ld_ffn, 16)
            sp.dma_start(wd_raw[:], w_down).then_inc(ld_ffn, 16)
            load_context(1, 1)
            load_x(1, 1)
            sp.wait_ge(invalid_ok, 1)
            load_mask(1)

            def spread(rows, width, slots, done, half):
                n = NB // 2 * width
                for j in range(J):
                    sp.dma_start(slots[half][32 * j:32 * j + 32, :, j].rearrange("p g b s -> p g (b s)").bitcast(F32),
                                 rows[32 * j:32 * j + 32, :, half * n:(half + 1) * n].bitcast(F32)) \
                        .then_inc(done[half], 16)

            def spread_quad(q, par, first=False):
                if first:
                    sp.wait_ge(pad_ok, 2)
                k_flat = k_rows[par][:].rearrange("p g b k -> p g (b k)")
                sp.wait_ge(krows_ok, G * (q + 1))
                spread(k_flat, KV, k_slots, kslots_ok, 0)
                sp.wait_ge(qrows_ok, G * (q + 1))
                spread(q_rows[par], S, q_slots, qslots_ok, 0)
                if first:
                    sp.wait_ge(pad_ok, 4)
                else:
                    sp.wait_ge(s_ps, G * NB * q)
                spread(k_flat, KV, k_slots, kslots_ok, 1)
                if not first:
                    sp.wait_ge(st_ps, G * NB * q)
                spread(q_rows[par], S, q_slots, qslots_ok, 1)

            spread_quad(0, 0, first=True)

            def step(k, par, ahead):
                q = 2 * k + par
                if ahead == 2:
                    sp.wait_ge(invalid_ok, q + 2)
                    load_mask(q + 2)
                    sp.wait_ge(ct_ps, q + 1)
                    load_context(q + 2, par)
                    load_x(q + 2, par)
                if ahead:
                    spread_quad(q + 1, 1 - par)

            quads(sp, step)

            with sp.Fori(0, QUADS) as q:
                sp.wait_ge(res_ok, RES0 + NB * (q + 1))
                sp.dma_start(out[bass.ds(q * NB, NB)].rearrange("b s d -> s b d"),
                             xs[:, bass.ds(q * NB + 1, NB), :]).then_inc(st_out, 16)
            sp.wait_ge(st_out, 16 * QUADS)

        @block.gpsimd
        def _(pool):
            pool.memset(ident[:], 0.0).then_inc(ident_zero, 1)
            pool.wait_ge(ident_zero, 1)
            pool.affine_select(out=ident[:], in_=ident[:], compare_op=ALU.not_equal, fill=1.0, base=0,
                               pattern=[[-1, 128]], channel_multiplier=1).then_inc(ident_ok, 1)
            pool.memset(ones[:], 1.0).then_inc(ones_ok, 1)
            pool.memset(minus_half[:], -0.5).then_inc(power_ok, 1)
            pool.memset(half[:], 0.5).then_inc(power_ok, 1)

            def diagonals(q):
                pool.wait_ge(fill_ok, NB * q + 1)
                for b in range(NB):
                    pool.tensor_tensor(diag[:, b, :], ident[0:KV, 0:KV],
                                       valid[:, bass.ds(q * NB + b, 1)].to_broadcast([KV, KV]), ALU.mult) \
                        .then_inc(diag_ok, 1)

            def deviations(q):
                pool.wait_ge(vareps_ok, q + 1)
                pool.tensor_tensor(rstd[:], var_eps[:], minus_half[:, 0:NB], ALU.pow).then_inc(rstd_ok, 1)

            def add_bias(q):
                pool.wait_ge(xn_ok, NB * (q + 1))
                pool.tensor_tensor(xs[:, bass.ds(q * NB + 1, NB), :], xs[:, bass.ds(q * NB + 1, NB), :],
                                   gated_bias[:].rearrange("p (o n) -> p o n", o=1).to_broadcast([S, NB, D]),
                                   ALU.add).then_inc(xb_ok, 1)

            pool.wait_ge(valid_ok, 1)
            diagonals(0)
            pool.wait_ge(power_ok, 2)
            deviations(0)
            pool.memset(k_slots[0][:].bitcast(F32), 0.0).then_inc(pad_ok, 1)
            diagonals(1)
            pool.memset(q_slots[0][:].bitcast(F32), 0.0).then_inc(pad_ok, 1)
            deviations(1)
            pool.memset(k_slots[1][:].bitcast(F32), 0.0).then_inc(pad_ok, 1)
            pool.memset(q_slots[1][:].bitcast(F32), 0.0).then_inc(pad_ok, 1)
            pool.memset(v_blocks[1], 0.0).then_inc(vzero_ok, 1)
            pool.wait_ge(gbias_ok, 1)
            add_bias(0)
            add_bias(1)

            def roots(n):
                cols = SEGMENTS[n]
                pool.wait_ge(moments2_ok, 5 * n + 4)
                pool.tensor_tensor(root[:, cols], var2[:, cols], half[:, cols], ALU.pow).then_inc(root_ok, 1)
                pool.wait_ge(moments2_ok, 5 * n + 5)
                pool.tensor_tensor(root_eps[:, cols], var2_eps[:, cols], half[:, cols], ALU.pow) \
                    .then_inc(root_ok, 1)

            def step(k, par, ahead):
                if ahead < 2:
                    roots(1 - ahead)
                if ahead == 2:
                    q = 2 * k + par + 2
                    diagonals(q)
                    deviations(q)
                    add_bias(q)

            quads(pool, step)

            def low_parts(q, par):
                for c in range(FS):
                    pool.wait_ge(hhi_ok, FS * q + c + 1)
                    pool.tensor_tensor(h_lo[par][:, c, :], act_h[par][:, c, :], h_hi[par][:, c, :].bitcast(F32),
                                       ALU.subtract).then_inc(hlo_ok, 1)

            low_parts(0, 0)
            roots(2)
            low_parts(1, 1)

            def stage(k, par, ahead):
                q = 2 * k + par
                pool.wait_ge(meansq_ok, MEANSQ0 + q + 1)
                pool.tensor_tensor(rms[:], mean_sq[:], half[:, 0:NB], ALU.pow).then_inc(rms_ok, 1)
                if ahead >= 2:
                    low_parts(q + 2, par)

            quads_deep(pool, stage)

        @block.scalar
        def _(act):
            act.wait_ge(ld_gates, 32)
            act.activation(tanh_g[:], gates[:], ACT.Tanh).then_inc(tanh_ok, 1)
            for n in range(3):
                act.wait_ge(wt_ps, n + 1)
                if n < 2:
                    act.activation(w_t[:, n, :], ps_s[n % 2][:, 0:D], ACT.Copy).then_inc(wt_ok, 1)
                else:
                    act.wait_ge(tanh_ok, 1)
                    act.activation(w_t[:, n, :], ps_s[n % 2][:, 0:D], ACT.Copy, scale=tanh_g[:, 0:1]) \
                        .then_inc(wt_ok, 1)

            def evacuate(task, q, par):
                bank = ps_p[task % 2]
                if task == 0:
                    act.wait_ge(xt_ps, q + 1)
                    act.activation(xn_t[:], bank[:], ACT.Copy).then_inc(xt_ok, 1)
                elif task == 1:
                    act.wait_ge(ct_ps, q + 1)
                    act.activation(context_t[:].rearrange("p b k -> p (b k)"), bank[:, 0:NB * KV], ACT.Copy) \
                        .then_inc(ct_ok, 1)
                elif task == 2:
                    act.wait_ge(q_ps, q + 1)
                    act.activation(q_hi[:], bank[:], ACT.Identity, bias=q_bias[:, 0:1]).then_inc(qhi_ok, 1)
                elif task == 3:
                    act.wait_ge(k_ps, q + 1)
                    act.activation(k_hi[:], bank[:, 0:NB * KV], ACT.Identity, bias=k_bias[:, 0:1]) \
                        .then_inc(khi_ok, 1)
                elif task > 8:
                    g = task - 9
                    act.wait_ge(qrows_ps, G * q + g + 1)
                    act.activation(q_rows[par][:, g, :], bank[:], ACT.Copy).then_inc(qrows_ok, 1)
                elif task > 4:
                    g = task - 5
                    act.wait_ge(krows_ps, G * q + g + 1)
                    act.activation(k_rows[par][:, g].rearrange("p b k -> p (b k)"), bank[:, 0:NB * KV], ACT.Copy) \
                        .then_inc(krows_ok, 1)

            act.wait_ge(ld_bias, 48)
            for task in range(NT):
                evacuate(task, 0, 0)
            for n, dst in enumerate((wu_t[:], wd_t[:].rearrange("p c d -> p (c d)"))):
                act.wait_ge(ternt_ps, n + 1)
                act.activation(dst, ps_st[n][:], ACT.Copy).then_inc(ternt_ok, 1)
            act.activation(att_t[:], ident[:, 0:1].to_broadcast([128, 2 * S]).rearrange("p (a b) -> p a b", a=2),
                           ACT.Identity, bias=1.0, scale=0.0).then_inc(o_ok, O0)

            def high_part(q):
                act.wait_ge(yt_ps, q + 1)
                act.activation(y_hi[:], ps_p[0][:], ACT.Copy).then_inc(yhi_ok, 1)

            def step(k, par, ahead):
                q = 2 * k + par
                for b in range(NB):
                    t = NB * q + b
                    if ahead == 0 and b == 3:
                        high_part(0)
                    for g in range(G):
                        act.wait_ge(st_ps, G * t + g + 1)
                        act.activation(probs[:, g].rearrange("p j s -> p (j s)"), ps_st[g % 2][0:KV, :], ACT.Exp,
                                       scale=SCALE).then_inc(exp_ok, 1)
                        if ahead and b < 3:
                            evacuate(G * b + g, q + 1, 1 - par)
                    if ahead and b == 2:
                        evacuate(NT - 1, q + 1, 1 - par)
                    if ahead == 0 and b == 3:
                        act.activation(gelu_warm[:], tanh_g[:, 0:1], ACT.Gelu)
                    act.wait_ge(o_ps, t + 1)
                    act.activation(att_t[:].rearrange("p a s -> p (a s)"), ps_o[:, 0:2 * S], ACT.Copy) \
                        .then_inc(o_ok, 1)

            quads(act, step)

            def gelus(q, par):
                for c in range(FC):
                    act.wait_ge(up_ps, FC * q + c + 1)
                    act.activation(act_h[par][:, c, :], up_banks[c][:], ACT.Gelu).then_inc(gelu_ok, 1)

            def square(q, par):
                act.wait_ge(sqsum_ok, SUM0 + q)
                for c in range(FC):
                    act.wait_ge(gelu_ok, GELU0 + FC * q + c + 1)
                    act.activation(squares[:, c, :], act_h[par][:, c, :], ACT.Square).then_inc(sq_ok, 1)

            gelus(0, 0)
            high_part(1)
            square(0, 0)

            def stage(k, par, ahead):
                q = 2 * k + par
                if ahead:
                    gelus(q + 1, 1 - par)
                if ahead == 2:
                    high_part(q + 2)
                if ahead:
                    square(q + 1, 1 - par)
                act.wait_ge(down_ps, q + 1)
                act.activation(ffn_t[:], ps_o[:], ACT.Copy).then_inc(ft_ok, 1)

            quads(act, stage)

        @block.tensor
        def _(pe):
            pe.wait_ge(ident_ok, 1)
            pe.wait_ge(maskf_ok, 1)
            pe.transpose(ps_o[0:KV, 0:B], mask_rows_f[:], ident[0:B, 0:B]).then_inc(maskt_ps, 1)
            pe.wait_ge(valid_ok, 1)
            pe.wait_ge(ones_ok, 1)
            pe.matmul(ps_t[0:KV, 0:B], ones[0:KV, 0:KV], valid[:], start=True, stop=True).then_inc(count_ps, 1)
            pe.wait_ge(ld_w, 48)
            for n in range(3):
                if n == 2:
                    pe.wait_ge(wt_ok, 1)
                pe.transpose(ps_s[n % 2][:, 0:D], w_raw[:, n, :], ident[:]).then_inc(wt_ps, 1)

            def prepare(task, k, par, first=False):
                q = 2 * k + par
                bank = ps_p[task % 2]
                if task == 0:
                    pe.wait_ge(xn_ok, NB * (q + 1))
                    if not first:
                        pe.wait_ge(qrows_ok, G * q)
                    for b in range(NB):
                        mm = pe.transpose(bank[:, b * S:(b + 1) * S], xn[:, b, :], ident[:])
                    mm.then_inc(xt_ps, 1)
                elif task == 1:
                    pe.wait_ge(fill_ok, NB * (q + 1) + 1)
                    pe.wait_ge(ld_ctx[par], 16 * (k + 1))
                    for b in range(NB):
                        mm = pe.matmul(bank[:, b * KV:(b + 1) * KV], context_in[:, par, b, :], fill[:, b, :],
                                       start=True, stop=True)
                    mm.then_inc(ct_ps, 1)
                elif task == 2:
                    if first:
                        pe.wait_ge(wt_ok, 3)
                    pe.wait_ge(xt_ok, q + 1)
                    pe.matmul(bank[:], w_t[:, 0, :], xn_t[:], start=True, stop=True).then_inc(q_ps, 1)
                elif task == 3:
                    pe.wait_ge(ct_ok, q + 1)
                    pe.matmul(bank[:, 0:NB * KV], w_t[:, 1, :], context_t[:].rearrange("p b k -> p (b k)"),
                              start=True, stop=True).then_inc(k_ps, 1)
                elif task == 4:
                    pe.wait_ge(qlo_ok, q + 1)
                    for b in range(NB):
                        mm = pe.matmul(bank[0:KV, b * D:(b + 1) * D], context_t[:, b, :], w_t[:, 2, :],
                                       start=True, stop=True)
                    mm.then_inc(v_ps, 1)
                elif task < 9:
                    g = task - 5
                    if g == 0:
                        pe.wait_ge(sel_ok, 1)
                        pe.wait_ge(khi_ok, q + 1)
                        pe.wait_ge(klo_ok, q + 1)
                    elif g == 1:
                        pe.wait_ge(v_ok, (G + 2) * (q + 1))
                    else:
                        pe.wait_ge(krows_ok, G * q + g - 1)
                    pe.matmul(bank[:, 0:NB * KV], select["k_hi_sel"][:, g, :], k_hi[:], start=True, stop=False)
                    pe.matmul(bank[:, 0:NB * KV], select["k_lo_sel"][:, g, :], k_lo[:], start=False, stop=True) \
                        .then_inc(krows_ps, 1)
                else:
                    g = task - 9
                    if g < 2:
                        pe.wait_ge(krows_ok, G * q + g + 3)
                    else:
                        pe.wait_ge(qrows_ok, G * q + g - 1)
                    pe.matmul(bank[:], select["q_hi_sel"][:, g, :], q_hi[:], start=True, stop=False)
                    pe.matmul(bank[:], select["q_lo_sel"][:, g, :], q_lo[:], start=False, stop=True) \
                        .then_inc(qrows_ps, 1)

            def scores(t, b, par, g, first=False):
                if g >= 2 or not first:
                    pe.wait_ge(max_ok, G * t + g - 1)
                pe.matmul(ps_s[g % 2][:, 0:J * KV], q_rows[par][:, g, b * S:(b + 1) * S],
                          k_slots[b // 2][:, g, :, b % 2, :], start=True, stop=True).then_inc(s_ps, 1)

            def shifted(t, b, par, g):
                pe.wait_ge(exp_ok, EXP0 + G * t + g - 1)
                pe.wait_ge(max_ok, G * t + g + 1)
                bank = ps_st[g % 2][0:KV, :]
                pe.matmul(bank, k_rows[par][:, g, b, :], q_slots[b // 2][:, g, :, b % 2, :], start=True, stop=False)
                for j in range(J):
                    mm = pe.matmul(bank[:, j * S:(j + 1) * S],
                                   neg_max[:, b % 2, J * g + j:J * g + j + 1].to_broadcast([S, KV]),
                                   ident_b[:], start=False, stop=(j == J - 1))
                mm.then_inc(st_ps, 1)

            def products(t, q, b, par, g):
                pe.wait_ge(exp_ok, EXP0 + G * t + g + 1)
                if g == 0:
                    pe.wait_ge(o_ok, O0 + t)
                    if b == 0:
                        pe.wait_ge(v_ok, (G + 2) * (q + 1))
                half_of = slice(0, S) if g < 3 else slice(S, 2 * S)
                for j in range(J):
                    mm = pe.matmul(ps_o[32 * j:32 * j + 32, half_of], v_blocks[par][:, b, J * g + j, :],
                                   probs[:, g, j, :], start=(g in (0, 3)), stop=(g in (2, 3)))
                if g == 3:
                    mm.then_inc(o_ps, 1)

            def turn_back(t):
                pe.wait_ge(o_ok, O0 + t)
                pe.wait_ge(x2_ok, X20 + t)
                for n in range(2):
                    mm = pe.transpose(ps_t[:, n * S:(n + 1) * S], att_t[:, n, :], ident[:])
                mm.then_inc(t_ps, 1)

            for task in range(NT):
                prepare(task, 0, 0, first=True)
            pe.wait_ge(abs_ok, 2)
            pe.matmul(ps_o[:, 0:2], ones[:], abs_sum[:], start=True, stop=True).then_inc(abs_ps, 1)
            pe.wait_ge(qrows_ok, G)
            pe.wait_ge(kslots_ok[0], 16 * J)
            for g in range(2):
                scores(0, 0, 0, g, first=True)
            pe.wait_ge(tern_ok, 2)
            for n in range(2):
                for c in range(FC):
                    mm = pe.transpose(ps_st[n][:, c * 128:(c + 1) * 128], tern[:, n, c * 128:(c + 1) * 128], ident[:])
                mm.then_inc(ternt_ps, 1)
            for g in range(2, G):
                scores(0, 0, 0, g)
            pe.wait_ge(ident_b_ok, 1)
            pe.wait_ge(share_ok, 1)
            pe.wait_ge(ternt_ok, 2)

            def turn_y(q):
                pe.wait_ge(y_ok, NB * (q + 1))
                for b in range(NB):
                    mm = pe.transpose(ps_p[0][:, b * S:(b + 1) * S], y[:, b, :], ident[:])
                mm.then_inc(yt_ps, 1)

            def step(k, par, ahead):
                q = 2 * k + par
                for b in range(NB):
                    t = NB * q + b
                    if ahead == 0 and b == 3:
                        turn_y(0)
                    if b % 2 == 0:
                        pe.wait_ge(qslots_ok[b // 2], 16 * J * (q + 1))
                    for g in range(G):
                        shifted(t, b, par, g)
                        if g:
                            products(t, q, b, par, g - 1)
                        if g == 1:
                            turn_back(t)
                        if b < 3:
                            if b == 1 and g == 0:
                                pe.wait_ge(kslots_ok[1], 16 * J * (q + 1))
                            scores(t + 1, b + 1, par, g)
                        elif ahead:
                            if g == 0:
                                pe.wait_ge(qrows_ok, G * (q + 2))
                                pe.wait_ge(kslots_ok[0], 16 * J * (q + 2))
                            scores(t + 1, 0, 1 - par, g)
                        if ahead and b < 3:
                            prepare(G * b + g, k + par, 1 - par)
                    if ahead and b == 2:
                        prepare(NT - 1, k + par, 1 - par)
                    products(t, q, b, par, 3)

            quads(pe, step)

            def up(q):
                pe.wait_ge(yhi_ok, q + 1)
                pe.wait_ge(ylo_ok, q + 1)
                for c in range(FC):
                    w = wu_t[:, c * 128:(c + 1) * 128]
                    pe.wait_ge(gelu_ok, FC * q + c + 1)
                    pe.matmul(up_banks[c][:], w, y_hi[:], start=True, stop=False)
                    pe.matmul(up_banks[c][:], w, y_lo[:], start=False, stop=True).then_inc(up_ps, 1)

            def sum_squares(b, par):
                return pe.matmul(ps_p[1][:, b:b + 1], square_sum[:, par, b * S:(b + 1) * S],
                                 ones[:, 0:1], start=True, stop=True)

            def down(q, par):
                pe.wait_ge(ft_ok, FT0 + q)
                for c in range(FS, FC):
                    pe.wait_ge(gelu_ok, GELU0 + FC * q + c + 1)
                    pe.matmul(ps_o[:], wd_t[:, c, :].bitcast(F32), act_h[par][:, c, :], start=(c == FS), stop=False)
                pe.wait_ge(sqsum_ok, SUM0 + q + 1)
                pe.wait_ge(meansq_ok, MEANSQ0 + q)
                for c in range(FS):
                    pe.wait_ge(hhi_ok, FS * q + c + 1)
                    pe.matmul(ps_o[:], wd_t[:, c, :], h_hi[par][:, c, :], start=False, stop=False)
                    pe.wait_ge(hlo_ok, FS * q + c + 1)
                    mm = pe.matmul(ps_o[:], wd_t[:, c, :], h_lo[par][:, c, :], start=False, stop=(c == FS - 1))
                    if c < FS - 1:
                        sum_squares(c, par)
                mm.then_inc(down_ps, 1)
                for b in range(FS - 1, NB):
                    mm = sum_squares(b, par)
                mm.then_inc(ssq_ps, 1)

            def turn_out(q):
                pe.wait_ge(ft_ok, FT0 + q + 1)
                pe.wait_ge(res_ok, RES0 + NB * q)
                for b in range(NB):
                    mm = pe.transpose(ps_t[:, b * D:(b + 1) * D], ffn_t[:, b * S:(b + 1) * S], ident[:])
                mm.then_inc(back_ps, 1)

            up(0)
            turn_back(B)
            turn_y(1)

            def stage(k, par, ahead):
                q = 2 * k + par
                if ahead:
                    up(q + 1)
                if ahead == 2:
                    turn_y(q + 2)
                down(q, par)
                turn_out(q)

            quads(pe, stage)

        @block.vector
        def _(dve):
            dve.wait_ge(ld_masks, 16)
            dve.tensor_copy(mask_rows_f[:], mask_rows[:]).then_inc(maskf_ok, 1)

            def ahead_of(k, par, piece, q_before=True):
                q = 2 * k + par
                if piece == 0:
                    dve.wait_ge(ld_mask, 16 * (q + 1))
                    dve.tensor_scalar(invalid[:].rearrange("p b k -> p (b k)"), mask_in[:], 0.0, None, ALU.is_equal) \
                        .then_inc(invalid_ok, 1)
                elif piece == 1:
                    dve.wait_ge(ld_x[par], 16 * (k + 1))
                    for b in range(NB):
                        dve.bn_stats(stats[:, b, :], xs[:, q * NB + b + 1, :]).then_inc(stats_ok, 1)
                elif piece in (2, 3):
                    if q_before:
                        dve.wait_ge(xt_ps, q)
                        dve.wait_ge(ct_ps, q)
                    dve.wait_ge(invalid_ok, q + 1)
                    dve.wait_ge(stats_ok, NB * (q + 1))
                    for b in range(2 * piece - 4, 2 * piece - 2):
                        dve.wait_ge(diag_ok, NB * q + b + 1)
                        dve.scalar_tensor_tensor(out=fill[:, b, :], in0=invalid[:, b, :],
                                                 scalar=valid_share[:, bass.ds(q * NB + b, 1)], in1=diag[:, b, :],
                                                 op0=ALU.mult, op1=ALU.add).then_inc(fill_ok, 1)
                elif piece == 4:
                    for b in range(NB):
                        dve.bn_aggr(moments[:, b, :], stats[:, b, :]).then_inc(moments_ok, 1)
                    dve.wait_ge(moments_ok, NB * (q + 1))
                    dve.tensor_scalar(var_eps[:], moments[:, :, 1], LN_EPS, None, ALU.add).then_inc(vareps_ok, 1)
                else:
                    dve.wait_ge(rstd_ok, q + 1)
                    for b in range(2 * piece - 10, 2 * piece - 8):
                        dve.tensor_scalar(xn[:, b, :], xs[:, q * NB + b + 1, :], moments[:, b, 0:1],
                                          rstd[:, b:b + 1], ALU.subtract, ALU.mult).then_inc(xn_ok, 1)

            piece_at = {(1, 1): 0, (1, 2): 1, (1, 3): 2, (2, 0): 4, (2, 1): 3, (2, 2): 5, (2, 3): 6}

            def evacuate(task, q, par):
                bank = ps_p[task % 2]
                if task == 2:
                    dve.wait_ge(qhi_ok, q + 1)
                    dve.scalar_tensor_tensor(out=q_lo[:], in0=bank[:], scalar=q_bias[:, 0:1],
                                             in1=q_hi[:].bitcast(F32), op0=ALU.add, op1=ALU.subtract) \
                        .then_inc(qlo_ok, 1)
                elif task == 3:
                    dve.wait_ge(khi_ok, q + 1)
                    dve.scalar_tensor_tensor(out=k_lo[:], in0=bank[:, 0:NB * KV], scalar=k_bias[:, 0:1],
                                             in1=k_hi[:].bitcast(F32), op0=ALU.add, op1=ALU.subtract) \
                        .then_inc(klo_ok, 1)
                elif task == 4:
                    dve.wait_ge(v_ps, q + 1)
                    dve.wait_ge(vzero_ok, par + 1)
                    keep = valid[:, bass.ds(q * NB, NB)]
                    for g in range(G):
                        dve.tensor_tensor(v_store[par][0:KV, :, J * g:J * g + J, (g % 3) * HD:(g % 3 + 1) * HD],
                                          bank[0:KV].rearrange("p (b g j i) -> p b g j i", b=NB, g=G, j=J)[:, :, g],
                                          keep.rearrange("p (b o n) -> p b o n", o=1, n=1).to_broadcast([KV, NB, J, HD]),
                                          ALU.mult).then_inc(v_ok, 1)
                    dve.tensor_copy(bass.AP(v_store[par], 24, [[NB * H * VC, KV], [H * VC, NB], [J * VC + 1, 3], [VC, J]]),
                                    keep.rearrange("p (b o n) -> p b o n", o=1, n=1).to_broadcast([KV, NB, 3, J])) \
                        .then_inc(v_ok, 1)
                    dve.tensor_copy(v_blocks[par][:, :, 12:16, 24],
                                    keep.rearrange("p (b o) -> p b o", o=1).to_broadcast([KV, NB, J])) \
                        .then_inc(v_ok, 1)

            def maximum(t, b, g):
                dve.wait_ge(s_ps, G * t + g + 1)
                dve.tensor_reduce(neg_max[:, b % 2, J * g:J * g + J],
                                  ps_s[g % 2][:, 0:J * KV].rearrange("p (j k) -> p j k", j=J),
                                  AX.X, ALU.max, negate=True).then_inc(max_ok, 1)

            def finish(t):
                tb = ps_t[:]
                dve.wait_ge(t_ps, t + 1)
                first = tb[:, 0:128].rearrange("p (j c) -> p j c", j=J)
                second = tb[:, 128:256].rearrange("p (j c) -> p j c", j=J)
                dve.reciprocal(inv_den[:, 0:12].rearrange("p (a j) -> p a j", a=3),
                               first[:, :, 24:27].rearrange("p j a -> p a j")).then_inc(den_ok, 1)
                dve.reciprocal(inv_den[:, 12:16], second[:, :, 24]).then_inc(den_ok, 1)
                dve.wait_ge(den_ok, 2 * t + 1)
                dve.tensor_tensor(att[:, 0:96].rearrange("p (a j i) -> p a j i", a=3, j=J),
                                  first[:, :, 0:24].rearrange("p j (a i) -> p a j i", a=3),
                                  inv_den[:, 0:12].rearrange("p (a j o) -> p a j o", a=3, o=1)
                                  .to_broadcast([S, 3, J, HD]), ALU.mult).then_inc(att_ok, 1)
                dve.wait_ge(den_ok, 2 * t + 2)
                dve.tensor_tensor(att[:, 96:128].rearrange("p (j i) -> p j i", j=J), second[:, :, 0:HD],
                                  inv_den[:, 12:16].rearrange("p (j o) -> p j o", o=1).to_broadcast([S, J, HD]),
                                  ALU.mult).then_inc(att_ok, 1)
                dve.wait_ge(att_ok, 2 * t + 2)
                dve.tensor_tensor(xs[:, t, :], xs[:, t, :], att[:], ALU.add).then_inc(x2_ok, 1)

            def measure(t):
                dve.bn_stats(stats2[:, t], xs[:, t, :]).then_inc(stats2_ok, 1)

            dve.wait_ge(maskt_ps, 1)
            dve.tensor_scalar(valid[:], ps_o[0:KV, 0:B], 0.0, None, ALU.not_equal).then_inc(valid_ok, 1)
            dve.memset(var2[:], 0.0).then_inc(fill_ok, 1)
            ahead_of(0, 0, 1)
            dve.wait_ge(count_ps, 1)
            dve.tensor_scalar(valid_n[:], ps_t[0:KV, 0:B], 1.0, None, ALU.max).then_inc(count_ok, 1)
            dve.wait_ge(stats_ok, NB)
            ahead_of(0, 0, 4)
            dve.wait_ge(count_ok, 1)
            dve.reciprocal(valid_share[:], valid_n[:]).then_inc(count_ok, 1)
            dve.wait_ge(count_ok, 2)
            dve.wait_ge(valid_ok, 1)
            dve.tensor_tensor(valid_share[:], valid_share[:], valid[:], ALU.mult).then_inc(share_ok, 1)
            ahead_of(0, 0, 0)
            ahead_of(0, 0, 5)
            ahead_of(0, 0, 6)
            dve.wait_ge(share_ok, 1)
            ahead_of(0, 0, 2, q_before=False)
            ahead_of(0, 0, 3, q_before=False)
            for n in select:
                dve.memset(select[n][:].bitcast(F32), 0.0).then_inc(sel_zero, 1)
            dve.wait_ge(sel_zero, 4)
            dve.wait_ge(ident_ok, 1)
            parts = {"q_hi_sel": (0, 1), "q_lo_sel": (2, 3), "k_hi_sel": (0, 2), "k_lo_sel": (1, 3)}
            for n, cs in parts.items():
                for c in cs:
                    last = dve.tensor_copy(
                        select[n][:].rearrange("p g (j c i) -> p g j c i", j=J, c=C)[:, :, :, c, :],
                        ident[:].rearrange("p (g j i) -> p g j i", g=G, j=J))
            last.then_inc(sel_ok, 1)
            dve.memset(v_blocks[0], 0.0).then_inc(vzero_ok, 1)
            evacuate(2, 0, 0)
            evacuate(3, 0, 0)
            evacuate(4, 0, 0)
            dve.wait_ge(tanh_ok, 1)
            dve.wait_ge(ld_bias, 48)
            dve.tensor_scalar(gated_bias[:], v_bias[:], tanh_g[:, 0:1], None, ALU.mult).then_inc(gbias_ok, 1)
            dve.tensor_copy(ident_b[:], ident[:]).then_inc(ident_b_ok, 1)
            for piece in range(5):
                ahead_of(0, 1, piece)

            dve.wait_ge(ld_ffn, 32)
            raws = [wu_raw[:].rearrange("p c d -> p (c d)"), wd_raw[:]]
            for n in range(2):
                dve.tensor_reduce(abs_sum[:, n:n + 1], raws[n], AX.X, ALU.add, apply_absolute_value=True) \
                    .then_inc(abs_ok, 1)
            ahead_of(0, 1, 5)
            ahead_of(0, 1, 6)
            dve.wait_ge(abs_ps, 1)
            dve.tensor_scalar(thresh[:], ps_o[:, 0:2], 1.0 / (F * D), 0.5, ALU.mult, ALU.mult).then_inc(thresh_ok, 1)
            dve.tensor_scalar(neg_thresh[:], ps_o[:, 0:2], 1.0 / (F * D), -0.5, ALU.mult, ALU.mult) \
                .then_inc(thresh_ok, 1)
            dve.wait_ge(thresh_ok, 2)
            for n in range(2):
                dve.tensor_scalar(tern_neg[:, n, :], raws[n], neg_thresh[:, n:n + 1], None, ALU.is_lt).then_inc(neg_ok, 1)
            for n in range(2):
                dve.wait_ge(neg_ok, n + 1)
                dve.scalar_tensor_tensor(out=tern[:, n, :], in0=raws[n], scalar=thresh[:, n:n + 1],
                                         in1=tern_neg[:, n, :], op0=ALU.is_gt, op1=ALU.subtract) \
                    .then_inc(tern_ok, 1)
            dve.memset(xs[:, 0, :], 0.0).then_inc(x2_ok, X20)
            dve.memset(inv_den[:], 0.0).then_inc(exp_ok, EXP0)
            dve.memset(out_scale[:], 0.0).then_inc(gelu_ok, GELU0)
            for g in range(G):
                maximum(0, 0, g)
            dve.wait_ge(x2_ok, X20)

            def moments_of(n):
                cols = SEGMENTS[n]
                dve.wait_ge(stats2_ok, cols.stop)
                even, odd = stats2[:, cols, 0], stats2[:, cols, 1]
                dve.tensor_tensor(mean2[:, cols], even[:, :, 1], odd[:, :, 1], ALU.add).then_inc(moments2_ok, 1)
                dve.tensor_tensor(mean_gap[:, cols], even[:, :, 1], odd[:, :, 1], ALU.subtract).then_inc(moments2_ok, 1)
                dve.tensor_tensor(var2[:, cols], even[:, :, 2], odd[:, :, 2], ALU.add).then_inc(moments2_ok, 1)
                dve.wait_ge(moments2_ok, 5 * n + 3)
                dve.tensor_scalar(mean2[:, cols], mean2[:, cols], 0.5, None, ALU.mult).then_inc(gap_ok, 1)
                dve.scalar_tensor_tensor(out=mean_gap[:, cols], in0=mean_gap[:, cols], scalar=0.25,
                                         in1=mean_gap[:, cols], op0=ALU.mult, op1=ALU.mult).then_inc(gap_ok, 1)
                dve.wait_ge(gap_ok, 2 * n + 2)
                dve.scalar_tensor_tensor(out=var2[:, cols], in0=var2[:, cols], scalar=1.0 / D, in1=mean_gap[:, cols],
                                         op0=ALU.mult, op1=ALU.add).then_inc(moments2_ok, 1)
                dve.wait_ge(moments2_ok, 5 * n + 4)
                dve.tensor_scalar(var2_eps[:, cols], var2[:, cols], LN_EPS, None, ALU.add).then_inc(moments2_ok, 1)

            def scales_of(n):
                cols = SEGMENTS[n]
                dve.wait_ge(root_ok, 2 * n + 2)
                dve.scalar_tensor_tensor(out=ffn_den[:, cols], in0=root_eps[:, cols], scalar=RMS_EPS,
                                         in1=root[:, cols], op0=ALU.mult, op1=ALU.add).then_inc(den2_ok, 1)
                dve.wait_ge(den2_ok, n + 1)
                dve.reciprocal(ffn_scale[:, cols], ffn_den[:, cols]).then_inc(scale2_ok, 1)

            def norm(q):
                for b in range(NB):
                    dve.tensor_scalar(y[:, b, :], xs[:, q * NB + b + 1, :],
                                      mean2[:, bass.ds(q * NB + b + 1, 1)], ffn_scale[:, bass.ds(q * NB + b + 1, 1)],
                                      ALU.subtract, ALU.mult).then_inc(y_ok, 1)

            def low_part(q):
                dve.wait_ge(yhi_ok, q + 1)
                dve.tensor_tensor(y_lo[:], ps_p[0][:], y_hi[:].bitcast(F32), ALU.subtract).then_inc(ylo_ok, 1)

            def step(k, par, ahead):
                q = 2 * k + par
                for b in range(NB):
                    t = NB * q + b
                    for g in range(G):
                        if g == 2:
                            dve.wait_ge(x2_ok, X20 + t + 1)
                        if b < 3 or ahead:
                            maximum(t + 1, b + 1, g)
                        if g == 2:
                            measure(t)
                        if ahead == 1 and (b, g) == (0, 3):
                            moments_of(0)
                        if ahead == 0 and (b, g) == (1, 0):
                            moments_of(1)
                        if ahead == 0 and (b, g) == (1, 3):
                            scales_of(0)
                        if ahead == 0 and (b, g) == (2, 2):
                            scales_of(1)
                        if ahead == 0 and (b, g) == (2, 3):
                            dve.wait_ge(scale2_ok, 1)
                            norm(0)
                        if ahead == 0 and (b, g) == (3, 1):
                            low_part(0)
                        if ahead == 0 and (b, g) == (3, 2):
                            dve.wait_ge(yt_ps, 1)
                            norm(1)
                        if ahead == 2 and (b, g) in piece_at:
                            ahead_of(k + 1, par, piece_at[b, g])
                        if ahead and b < 3:
                            evacuate(G * b + g, q + 1, 1 - par)
                        if g == 1:
                            if b == 1:
                                dve.wait_ge(xb_ok, q + 1)
                            finish(t)

            quads(dve, step)
            dve.memset(square_sum[:], 0.0).then_inc(sqsum_ok, SUM0)
            dve.memset(rms_inv[:], 0.0).then_inc(res_ok, RES0)
            dve.memset(mean_sq[:], 0.0).then_inc(meansq_ok, MEANSQ0)
            dve.memset(out_scale[:], 0.0).then_inc(ft_ok, FT0)
            finish(B)
            dve.wait_ge(x2_ok, X20 + B + 1)
            measure(B)
            moments_of(2)

            def high_parts(q, par):
                for c in range(FS):
                    dve.wait_ge(gelu_ok, GELU0 + FC * q + c + 1)
                    dve.tensor_copy(h_hi[par][:, c, :], act_h[par][:, c, :]).then_inc(hhi_ok, 1)

            def add_squares(q, par):
                for n in range(2):
                    dve.wait_ge(sq_ok, FC * q + 2 * n + 2)
                    dve.tensor_tensor(pair_sum[:, n, :], squares[:, 2 * n, :], squares[:, 2 * n + 1, :], ALU.add) \
                        .then_inc(pairs_ok, 1)
                dve.wait_ge(pairs_ok, 2 * q + 2)
                dve.tensor_tensor(square_sum[:, par, :], pair_sum[:, 0, :], pair_sum[:, 1, :], ALU.add) \
                    .then_inc(sqsum_ok, 1)

            high_parts(0, 0)
            low_part(1)
            dve.wait_ge(yt_ps, 2)
            norm(2)
            add_squares(0, 0)
            scales_of(2)
            high_parts(1, 1)
            low_part(2)
            add_squares(1, 1)
            dve.wait_ge(scale2_ok, 3)

            def stage(k, par, ahead):
                q = 2 * k + par
                dve.wait_ge(ssq_ps, q + 1)
                dve.tensor_scalar(mean_sq[:], ps_p[1][:, 0:NB], 1.0 / F, None, ALU.mult) \
                    .then_inc(meansq_ok, 1)
                if ahead == 3:
                    dve.wait_ge(yt_ps, q + 3)
                    norm(q + 3)
                dve.wait_ge(rms_ok, q + 1)
                dve.tensor_scalar(rms_inv[:], rms[:], RMS_EPS, None, ALU.add).then_inc(rmse_ok, 1)
                dve.wait_ge(rmse_ok, q + 1)
                dve.reciprocal(rms_inv[:], rms_inv[:]).then_inc(rinv_ok, 1)
                dve.wait_ge(rinv_ok, q + 1)
                dve.tensor_scalar(out_scale[:], rms_inv[:], tanh_g[:, 1:2], None, ALU.mult).then_inc(oscale_ok, 1)
                dve.wait_ge(oscale_ok, q + 1)
                dve.wait_ge(back_ps, q + 1)
                for b in range(NB):
                    dve.scalar_tensor_tensor(out=xs[:, q * NB + b + 1, :], in0=ps_t[:, b * D:(b + 1) * D],
                                             scalar=out_scale[:, b:b + 1], in1=xs[:, q * NB + b + 1, :],
                                             op0=ALU.mult, op1=ALU.add).then_inc(res_ok, 1)
                if ahead >= 2:
                    high_parts(q + 2, par)
                if ahead == 3:
                    low_part(q + 3)
                if ahead >= 2:
                    add_squares(q + 2, par)

            quads_deep(dve, stage)


_INS = ["x", "ctx_1024", "mask_Bx1x1xS2_ik0", "g_xattn", "g_ffn", "L0_xattn_Wq", "L0_xattn_bq", "L0_xattn_Wk",
        "L0_xattn_bk", "L0_xattn_Wv", "L0_xattn_bv", "L0_ffn_w_up", "L0_ffn_w_down"]


def kernel(**inputs):
    import numpy as np
    import concourse.bacc as bacc
    from concourse.bass_utils import run_bass_kernel_spmd

    nc = bacc.Bacc("TRN2", target_bir_lowering=False, num_devices=1)
    arrays, args = {}, []
    for name in _INS:
        a = np.ascontiguousarray(inputs[name])
        if name.startswith("mask"):
            a = a.reshape(B, KV)
        arrays[f"in_{name}"] = a
        args.append(nc.dram_tensor(f"in_{name}", a.shape, mybir.dt.from_np(a.dtype), kind="ExternalInput").ap())
    out = nc.dram_tensor("out_0", (B, S, D), F32, kind="ExternalOutput").ap()
    flamingo_kernel(nc, *args, out)
    r = run_bass_kernel_spmd(nc, [arrays], core_ids=[0])
    return r.results[0]["out_0"]
```

```python
from contextlib import ExitStack

import concourse.bass as bass
from concourse import mybir

F32 = mybir.dt.float32
F32R = mybir.dt.float32r
BF16 = mybir.dt.bfloat16
I32 = mybir.dt.int32
ALU = mybir.AluOpType
ACT = mybir.ActivationFunctionType
AX = mybir.AxisListType

B, S, D = 32, 128, 128
KV = 120
H, HD = 16, 8
F = 512
NB = 4
QUADS = B // NB
G, J = 4, 4
C = 4
FC = F // 128
FS = 3
LN_EPS = 1e-5
RMS_EPS = 1e-8
SCALE = float(HD) ** -0.5
VC = 32


def flamingo_kernel(nc, x, context, mask, g_xattn, g_ffn, wq, bq, wk, bk, wv, bv, w_up, w_down, out):
    ctx = ExitStack()
    with ctx:
        def sb(name, shape, dt=F32):
            return ctx.enter_context(nc.sbuf_tensor(name, shape, dt))

        def psum(name, shape):
            return ctx.enter_context(nc.psum_tensor(name, shape, F32))

        def sem(name):
            return ctx.enter_context(nc.semaphore(name))

        xs = sb("xs", [S, B + 1, D])
        ident = sb("ident", [128, 128])
        ident_b = sb("ident_b", [128, 128], BF16)
        ones = sb("ones", [128, 128])
        select = {n: sb(n, [128, G, 128], F32R) for n in ("q_hi_sel", "q_lo_sel", "k_hi_sel", "k_lo_sel")}
        w_raw = sb("w_raw", [128, 3, D])
        w_t = sb("w_t", [128, 3, D])
        q_bias = sb("q_bias", [128, 1])
        k_bias = sb("k_bias", [128, 1])
        v_bias = sb("v_bias", [128, D])
        gates = sb("gates", [128, 2])
        tanh_g = sb("tanh_g", [128, 2])
        gated_bias = sb("gated_bias", [128, D])
        mask_rows = sb("mask_rows", [B, KV], I32)
        mask_rows_f = sb("mask_rows_f", [B, KV])
        valid = sb("valid", [KV, B])
        valid_n = sb("valid_n", [KV, B])
        valid_share = sb("valid_share", [KV, B])
        minus_half = sb("minus_half", [128, B + 1])
        half = sb("half", [128, B + 1])

        context_in = sb("context_in", [KV, 2, NB, D])
        mask_in = sb("mask_in", [KV, NB * KV], I32)
        invalid = sb("invalid", [KV, NB, KV])
        diag = sb("diag", [KV, NB, KV])
        fill = sb("fill", [KV, NB, KV])
        stats = sb("stats", [S, NB, 6])
        moments = sb("moments", [S, NB, 2])
        var_eps = sb("var_eps", [S, NB])
        rstd = sb("rstd", [S, NB])
        xn = sb("xn", [S, NB, D])
        xn_t = sb("xn_t", [D, NB * S])
        context_t = sb("context_t", [D, NB, KV])
        q_hi = sb("q_hi", [128, NB * S], F32R)
        q_lo = sb("q_lo", [128, NB * S], F32R)
        k_hi = sb("k_hi", [128, NB * KV], F32R)
        k_lo = sb("k_lo", [128, NB * KV], F32R)
        q_rows = [sb(f"q_rows{p}", [128, G, NB * S], F32R) for p in range(2)]
        k_rows = [sb(f"k_rows{p}", [128, G, NB, KV], F32R) for p in range(2)]
        q_slots = [sb(f"q_slots{p}", [128, G, J, NB // 2, S], F32R) for p in range(2)]
        k_slots = [sb(f"k_slots{p}", [128, G, J, NB // 2, KV], F32R) for p in range(2)]
        v_store = [sb(f"v_blocks{p}", [128, NB, H, VC]) for p in range(2)]
        v_blocks = [v[0:KV] for v in v_store]
        neg_max = sb("neg_max", [S, 2, H], BF16)
        p_store = sb("probs", [128, G, J, S])
        probs = p_store[0:KV]
        att_t = sb("att_t", [128, 2, S])
        inv_den = sb("inv_den", [S, H])
        att = sb("att", [S, D])
        stats2 = sb("stats2", [S, B + 1, 2, 3])
        mean2 = sb("mean2", [S, B + 1])
        mean_gap = sb("mean_gap", [S, B + 1])
        var2 = sb("var2", [S, B + 1])
        root = sb("root", [S, B + 1])
        var2_eps = sb("var2_eps", [S, B + 1])
        root_eps = sb("root_eps", [S, B + 1])
        ffn_den = sb("ffn_den", [S, B + 1])
        ffn_scale = sb("ffn_scale", [S, B + 1])

        wu_raw = sb("wu_raw", [128, FC, D])
        wd_raw = sb("wd_raw", [D, F])
        tern = sb("tern", [128, 2, F])
        tern_neg = sb("tern_neg", [128, 2, F])
        abs_sum = sb("abs_sum", [128, 2])
        thresh = sb("thresh", [128, 2])
        neg_thresh = sb("neg_thresh", [128, 2])
        wu_t = sb("wu_t", [D, F], F32R)
        wd_t = sb("wd_t", [128, FC, D], F32R)
        y = sb("y", [S, NB, D])
        y_hi, y_lo = q_hi, q_lo
        act_h = [v[:].rearrange("p b h c -> p (b h c)").rearrange("p (c n) -> p c n", c=FC) for v in v_store]
        squares = p_store[:].rearrange("p g j s -> p g (j s)")
        h_hi = [r[:, 0:FS, :] for r in q_rows]
        h_lo = [k[:].rearrange("p g j b k -> p (g j b k)")[:, 0:FS * NB * S].rearrange("p (c n) -> p c n", c=FS)
                for k in k_slots]
        ffn_t = sb("ffn_t", [D, NB * S])
        square_sum = sb("square_sum", [128, 2, NB * S])
        pair_sum = sb("pair_sum", [128, 2, NB * S])
        gelu_warm = sb("gelu_warm", [128, 1])
        mean_sq = sb("mean_sq", [S, NB])
        rms = sb("rms", [S, NB])
        rms_inv = sb("rms_inv", [S, NB])
        rms_eps = sb("rms_eps", [S, NB])
        eps = sb("eps", [S, NB])

        ps_s = [psum(f"ps_s{i}", [128, 512]) for i in range(2)]
        ps_st = [psum(f"ps_st{i}", [128, 512]) for i in range(2)]
        ps_o = psum("ps_o", [128, 512])
        ps_t = psum("ps_t", [128, 512])
        ps_p = [psum(f"ps_p{i}", [128, 512]) for i in range(2)]

        ld_x = [sem(f"ld_x{p}") for p in range(2)]
        ld_w = sem("ld_w")
        ld_masks = sem("ld_masks")
        ld_gates = sem("ld_gates")
        ld_bias = sem("ld_bias")
        ld_ctx = [sem(f"ld_ctx{p}") for p in range(2)]
        ld_mask = sem("ld_mask")
        ld_ffn = sem("ld_ffn")
        ident_zero = sem("ident_zero")
        ident_ok = sem("ident_ok")
        ident_b_ok = sem("ident_b_ok")
        ones_ok = sem("ones_ok")
        power_ok = sem("power_ok")
        vzero_ok = sem("vzero_ok")
        sel_zero = sem("sel_zero")
        sel_ok = sem("sel_ok")
        pad_ok = sem("pad_ok")
        tanh_ok = sem("tanh_ok")
        gbias_ok = sem("gbias_ok")
        wt_ps = sem("wt_ps")
        wt_ok = sem("wt_ok")
        maskf_ok = sem("maskf_ok")
        maskt_ps = sem("maskt_ps")
        valid_ok = sem("valid_ok")
        count_ps = sem("count_ps")
        count_ok = sem("count_ok")
        share_ok = sem("share_ok")
        stats_ok = sem("stats_ok")
        moments_ok = sem("moments_ok")
        vareps_ok = sem("vareps_ok")
        rstd_ok = sem("rstd_ok")
        xn_ok = sem("xn_ok")
        xb_ok = sem("xb_ok")
        invalid_ok = sem("invalid_ok")
        diag_ok = sem("diag_ok")
        fill_ok = sem("fill_ok")
        xt_ps = sem("xt_ps")
        xt_ok = sem("xt_ok")
        ct_ps = sem("ct_ps")
        ct_ok = sem("ct_ok")
        q_ps = sem("q_ps")
        qhi_ok = sem("qhi_ok")
        qlo_ok = sem("qlo_ok")
        k_ps = sem("k_ps")
        khi_ok = sem("khi_ok")
        klo_ok = sem("klo_ok")
        v_ps = sem("v_ps")
        v_ok = sem("v_ok")
        qrows_ps = sem("qrows_ps")
        qrows_ok = sem("qrows_ok")
        qslots_ok = [sem(f"qslots_ok{p}") for p in range(2)]
        kslots_ok = [sem(f"kslots_ok{p}") for p in range(2)]
        krows_ps = sem("krows_ps")
        krows_ok = sem("krows_ok")
        s_ps = sem("s_ps")
        max_ok = sem("max_ok")
        st_ps = sem("st_ps")
        exp_ok = sem("exp_ok")
        o_ps = sem("o_ps")
        o_ok = sem("o_ok")
        t_ps = sem("t_ps")
        den_ok = sem("den_ok")
        att_ok = sem("att_ok")
        x2_ok = sem("x2_ok")
        stats2_ok = sem("stats2_ok")
        moments2_ok = sem("moments2_ok")
        gap_ok = sem("gap_ok")
        root_ok = sem("root_ok")
        den2_ok = sem("den2_ok")
        scale2_ok = sem("scale2_ok")
        abs_ok = sem("abs_ok")
        abs_ps = sem("abs_ps")
        thresh_ok = sem("thresh_ok")
        neg_ok = sem("neg_ok")
        tern_ok = sem("tern_ok")
        ternt_ps = sem("ternt_ps")
        ternt_ok = sem("ternt_ok")
        y_ok = sem("y_ok")
        yt_ps = sem("yt_ps")
        yhi_ok = sem("yhi_ok")
        ylo_ok = sem("ylo_ok")
        hhi_ok = sem("hhi_ok")
        hlo_ok = sem("hlo_ok")
        ft_ok = sem("ft_ok")
        back_ps = sem("back_ps")
        up_ps = sem("up_ps")
        gelu_ok = sem("gelu_ok")
        sq_ok = sem("sq_ok")
        sqsum_ok = sem("sqsum_ok")
        down_ps = sem("down_ps")
        ssq_ps = sem("ssq_ps")
        meansq_ok = sem("meansq_ok")
        rms_ok = sem("rms_ok")
        rmse_ok = sem("rmse_ok")
        pairs_ok = sem("pairs_ok")
        rinv_ok = sem("rinv_ok")
        res_ok = sem("res_ok")
        st_out = sem("st_out")

        EXP0, O0, X20 = 2, 1, 1
        GELU0, SUM0, MEANSQ0, FT0, RES0 = FC, 1, 1, 1, 1

        up_banks = ps_s + ps_st

        XT, CT, QP, KP, VP = "x", "context", "Q", "K", "V"
        QR = ["Q's rows 0", "Q's rows 1", "Q's rows 2", "Q's rows 3"]
        KR = ["K's rows 0", "K's rows 1", "K's rows 2", "K's rows 3"]
        tasks_at = {(0, 0): (XT,), (0, 1): (CT, QP), (0, 2): (KP,), (0, 3): (QR[0],),
                    (1, 0): (KR[0],), (1, 1): (KR[1],), (1, 2): (KR[2],), (1, 3): (KR[3],),
                    (2, 0): (QR[1],), (2, 1): (QR[2],), (2, 2): (QR[3],), (3, 3): (VP,)}
        bank_of = {XT: ps_p[1], CT: ps_p[0], QP: ps_p[1], KP: ps_p[0], QR[0]: ps_p[1], KR[0]: ps_p[0],
                   KR[1]: ps_p[1], KR[2]: ps_p[0], KR[3]: ps_p[1], QR[1]: ps_p[0], QR[2]: ps_p[1],
                   QR[3]: ps_p[0], VP: ps_p[0]}
        first_tasks = (CT, XT, KP, QP, *KR, *QR, VP)
        first_bank_of = dict(zip(first_tasks, (ps_p[1], ps_p[0], ps_st[1], ps_st[0], ps_p[0], ps_p[1],
                                               ps_s[0], ps_s[1], ps_st[0], ps_st[1], ps_t, ps_o, ps_p[0])))

        SEGMENTS = (slice(0, B + 1 - 2 * NB), slice(B + 1 - 2 * NB, B + 1 - NB), slice(B + 1 - NB, B + 1))

        block = ctx.enter_context(nc.Block())

        def quads(eng, step):
            with eng.Fori(0, QUADS // 2 - 1) as it:
                for par in range(2):
                    step(it, par, 2)
            step(QUADS // 2 - 1, 0, 1)
            step(QUADS // 2 - 1, 1, 0)

        def quads_deep(eng, step):
            with eng.Fori(0, QUADS // 2 - 2) as it:
                for par in range(2):
                    step(it, par, 3)
            for last in range(4):
                step(QUADS // 2 - 2 + last // 2, last % 2, 3 - last)

        @block.sync
        def _(sp):
            def load_x(q, par):
                sp.dma_start(xs[:, bass.ds(q * NB + 1, NB), :], x[bass.ds(q * NB, NB)].rearrange("b s d -> s b d")) \
                    .then_inc(ld_x[par], 16)

            sp.dma_start(mask_rows[:], mask).then_inc(ld_masks, 16)
            load_x(0, 0)
            sp.dma_start(context_in[:, 0], context[0:NB].rearrange("b k d -> k b d")).then_inc(ld_ctx[0], 16)
            sp.dma_start(mask_in[:], mask[0:NB].rearrange("b k -> (b k)").rearrange("(o n) -> o n", o=1)
                         .to_broadcast([KV, NB * KV])).then_inc(ld_mask, 16)
            for n, w in enumerate((wq, wk, wv)):
                sp.dma_start(w_raw[:, n, :], w).then_inc(ld_w, 16)
            for n, g in enumerate((g_xattn, g_ffn)):
                sp.dma_start(gates[:, n:n + 1], g.rearrange("(o n) -> o n", o=1).to_broadcast([128, 1])) \
                    .then_inc(ld_gates, 16)

            def load_context(q, par):
                sp.dma_start(context_in[:, par], context[bass.ds(q * NB, NB)].rearrange("b k d -> k b d")) \
                    .then_inc(ld_ctx[par], 16)

            def load_mask(q):
                sp.dma_start(mask_in[:], mask[bass.ds(q * NB, NB)].rearrange("b k -> (b k)")
                             .rearrange("(o n) -> o n", o=1).to_broadcast([KV, NB * KV])).then_inc(ld_mask, 16)

            sp.dma_start(q_bias[:], bq.rearrange("(p o) -> p o", o=1)).then_inc(ld_bias, 16)
            sp.dma_start(k_bias[:], bk.rearrange("(p o) -> p o", o=1)).then_inc(ld_bias, 16)
            sp.dma_start(v_bias[:], bv.rearrange("(o n) -> o n", o=1).to_broadcast([128, D])).then_inc(ld_bias, 16)
            sp.dma_start(wu_raw[:], w_up.rearrange("(c p) d -> p c d", p=128)).then_inc(ld_ffn, 16)
            sp.dma_start(wd_raw[:], w_down).then_inc(ld_ffn, 16)
            load_context(1, 1)
            load_x(1, 1)
            sp.wait_ge(invalid_ok, 1)
            load_mask(1)

            def spread(rows, width, slots, done, half):
                n = NB // 2 * width
                for j in range(J):
                    sp.dma_start(slots[half][32 * j:32 * j + 32, :, j].rearrange("p g b s -> p g (b s)").bitcast(F32),
                                 rows[32 * j:32 * j + 32, :, half * n:(half + 1) * n].bitcast(F32)) \
                        .then_inc(done[half], 16)

            def spread_quad(q, par, first=False):
                if first:
                    sp.wait_ge(pad_ok, 1)
                k_flat = k_rows[par][:].rearrange("p g b k -> p g (b k)")
                sp.wait_ge(krows_ok, G * (q + 1))
                spread(k_flat, KV, k_slots, kslots_ok, 0)
                if first:
                    sp.wait_ge(pad_ok, 2)
                sp.wait_ge(qrows_ok, G * (q + 1))
                spread(q_rows[par], S, q_slots, qslots_ok, 0)
                if first:
                    sp.wait_ge(pad_ok, 3)
                else:
                    sp.wait_ge(s_ps, G * NB * q)
                spread(k_flat, KV, k_slots, kslots_ok, 1)
                if first:
                    sp.wait_ge(pad_ok, 4)
                else:
                    sp.wait_ge(st_ps, G * NB * q)
                spread(q_rows[par], S, q_slots, qslots_ok, 1)

            spread_quad(0, 0, first=True)

            def step(k, par, ahead):
                q = 2 * k + par
                if ahead == 2:
                    sp.wait_ge(invalid_ok, q + 2)
                    load_mask(q + 2)
                    sp.wait_ge(ct_ps, q + 1)
                    load_context(q + 2, par)
                    load_x(q + 2, par)
                if ahead:
                    spread_quad(q + 1, 1 - par)

            quads(sp, step)

            with sp.Fori(0, QUADS - 1) as q:
                sp.wait_ge(res_ok, RES0 + NB * (q + 1))
                sp.dma_start(out[bass.ds(q * NB, NB)].rearrange("b s d -> s b d"),
                             xs[:, bass.ds(q * NB + 1, NB), :]).then_inc(st_out, 16)
            for b in (B - NB, B - NB // 2):
                sp.wait_ge(res_ok, RES0 + b + NB // 2)
                sp.dma_start(out[b:b + NB // 2].rearrange("b s d -> s b d"), xs[:, b + 1:b + 1 + NB // 2, :]) \
                    .then_inc(st_out, 16)
            sp.wait_ge(st_out, 16 * (QUADS + 1))

        @block.gpsimd
        def _(pool):
            pool.memset(ident[:], 0.0).then_inc(ident_zero, 1)
            pool.wait_ge(ident_zero, 1)
            pool.affine_select(out=ident[:], in_=ident[:], compare_op=ALU.not_equal, fill=1.0, base=0,
                               pattern=[[-1, 128]], channel_multiplier=1).then_inc(ident_ok, 1)
            pool.memset(ones[:], 1.0).then_inc(ones_ok, 1)
            pool.memset(minus_half[:], -0.5).then_inc(power_ok, 1)
            pool.memset(half[:], 0.5).then_inc(power_ok, 1)
            pool.memset(eps[:], RMS_EPS).then_inc(power_ok, 1)

            def diagonals(q):
                pool.wait_ge(fill_ok, NB * q + 1)
                for b in range(NB):
                    pool.tensor_tensor(diag[:, b, :], ident[0:KV, 0:KV],
                                       valid[:, bass.ds(q * NB + b, 1)].to_broadcast([KV, KV]), ALU.mult) \
                        .then_inc(diag_ok, 1)

            def deviations(q):
                pool.wait_ge(vareps_ok, q + 1)
                pool.tensor_tensor(rstd[:], var_eps[:], minus_half[:, 0:NB], ALU.pow).then_inc(rstd_ok, 1)

            def add_bias(q):
                pool.wait_ge(xn_ok, NB * (q + 1))
                pool.tensor_tensor(xs[:, bass.ds(q * NB + 1, NB), :], xs[:, bass.ds(q * NB + 1, NB), :],
                                   gated_bias[:].rearrange("p (o n) -> p o n", o=1).to_broadcast([S, NB, D]),
                                   ALU.add).then_inc(xb_ok, 1)

            pool.wait_ge(valid_ok, 1)
            diagonals(0)
            pool.wait_ge(power_ok, 3)
            deviations(0)
            pool.memset(k_slots[0][:].bitcast(F32), 0.0).then_inc(pad_ok, 1)
            pool.memset(q_slots[0][:].bitcast(F32), 0.0).then_inc(pad_ok, 1)
            diagonals(1)
            pool.memset(k_slots[1][:].bitcast(F32), 0.0).then_inc(pad_ok, 1)
            deviations(1)
            pool.memset(q_slots[1][:].bitcast(F32), 0.0).then_inc(pad_ok, 1)
            pool.wait_ge(gbias_ok, 1)
            add_bias(0)
            pool.memset(v_blocks[1], 0.0).then_inc(vzero_ok, 1)
            add_bias(1)

            def roots(n):
                cols = SEGMENTS[n]
                pool.wait_ge(moments2_ok, 5 * n + 4)
                pool.tensor_tensor(root[:, cols], var2[:, cols], half[:, cols], ALU.pow).then_inc(root_ok, 1)
                pool.wait_ge(moments2_ok, 5 * n + 5)
                pool.tensor_tensor(root_eps[:, cols], var2_eps[:, cols], half[:, cols], ALU.pow) \
                    .then_inc(root_ok, 1)

            def step(k, par, ahead):
                if ahead < 2:
                    roots(1 - ahead)
                if ahead == 2:
                    q = 2 * k + par + 2
                    diagonals(q)
                    deviations(q)
                    add_bias(q)

            quads(pool, step)

            def low_parts(q, par):
                for c in range(FS):
                    pool.wait_ge(hhi_ok, FS * q + c + 1)
                    pool.tensor_tensor(h_lo[par][:, c, :], act_h[par][:, c, :], h_hi[par][:, c, :].bitcast(F32),
                                       ALU.subtract).then_inc(hlo_ok, 1)

            low_parts(0, 0)
            roots(2)
            low_parts(1, 1)

            def stage(k, par, ahead):
                q = 2 * k + par
                pool.wait_ge(meansq_ok, MEANSQ0 + q + 1)
                pool.tensor_tensor(rms[:], mean_sq[:], half[:, 0:NB], ALU.pow).then_inc(rms_ok, 1)
                pool.wait_ge(rms_ok, q + 1)
                pool.tensor_tensor(rms_eps[:], rms[:], eps[:], ALU.add).then_inc(rmse_ok, 1)
                if ahead >= 2:
                    low_parts(q + 2, par)

            quads_deep(pool, stage)

        @block.scalar
        def _(act):
            act.wait_ge(ident_ok, 1)

            def zero(tile, n):
                rows = tile.shape[0]
                return act.activation(tile, ident[0:rows, 0:1].to_broadcast([rows, n]), ACT.Copy, scale=0.0)

            for n in select:
                zero(select[n][:].rearrange("p g m -> p (g m)"), G * 128).then_inc(sel_zero, 1)
            zero(v_blocks[0].rearrange("p b h c -> p (b h c)"), NB * H * VC).then_inc(vzero_ok, 1)
            act.wait_ge(ld_gates, 32)
            act.activation(tanh_g[:], gates[:], ACT.Tanh).then_inc(tanh_ok, 1)
            for n in range(3):
                act.wait_ge(wt_ps, n + 1)
                if n < 2:
                    act.activation(w_t[:, n, :], ps_s[n % 2][:, 0:D], ACT.Copy).then_inc(wt_ok, 1)
                else:
                    act.wait_ge(tanh_ok, 1)
                    act.activation(w_t[:, n, :], ps_s[n % 2][:, 0:D], ACT.Copy, scale=tanh_g[:, 0:1]) \
                        .then_inc(wt_ok, 1)

            def evacuate(task, q, par, bank):
                if task == XT:
                    act.wait_ge(xt_ps, q + 1)
                    act.activation(xn_t[:], bank[:], ACT.Copy).then_inc(xt_ok, 1)
                elif task == CT:
                    act.wait_ge(ct_ps, q + 1)
                    act.activation(context_t[:].rearrange("p b k -> p (b k)"), bank[:, 0:NB * KV], ACT.Copy) \
                        .then_inc(ct_ok, 1)
                elif task == QP:
                    act.wait_ge(q_ps, q + 1)
                    act.activation(q_hi[:], bank[:], ACT.Identity, bias=q_bias[:, 0:1]).then_inc(qhi_ok, 1)
                elif task == KP:
                    act.wait_ge(k_ps, q + 1)
                    act.activation(k_hi[:], bank[:, 0:NB * KV], ACT.Identity, bias=k_bias[:, 0:1]) \
                        .then_inc(khi_ok, 1)
                elif task in KR:
                    g = KR.index(task)
                    act.wait_ge(krows_ps, G * q + g + 1)
                    act.activation(k_rows[par][:, g].rearrange("p b k -> p (b k)"), bank[:, 0:NB * KV], ACT.Copy) \
                        .then_inc(krows_ok, 1)
                elif task in QR:
                    g = QR.index(task)
                    act.wait_ge(qrows_ps, G * q + g + 1)
                    act.activation(q_rows[par][:, g, :], bank[:], ACT.Copy).then_inc(qrows_ok, 1)

            act.wait_ge(ld_bias, 48)
            for task in (CT, XT, KP, QP, KR[0], KR[2], QR[0], QR[2]):
                evacuate(task, 0, 0, first_bank_of[task])
            act.activation(att_t[:], ident[:, 0:1].to_broadcast([128, 2 * S]).rearrange("p (a b) -> p a b", a=2),
                           ACT.Identity, bias=1.0, scale=0.0).then_inc(o_ok, O0)

            def high_part(q):
                act.wait_ge(yt_ps, q + 1)
                act.activation(y_hi[:], ps_p[0][:], ACT.Copy).then_inc(yhi_ok, 1)

            def step(k, par, ahead):
                q = 2 * k + par
                for b in range(NB):
                    t = NB * q + b
                    if ahead == 0 and b == 3:
                        for n, dst in enumerate((wu_t[:], wd_t[:].rearrange("p c d -> p (c d)"))):
                            act.wait_ge(ternt_ps, n + 1)
                            act.activation(dst, ps_p[n][:], ACT.Copy).then_inc(ternt_ok, 1)
                    for g in range(G):
                        act.wait_ge(st_ps, G * t + g + 1)
                        act.activation(probs[:, g].rearrange("p j s -> p (j s)"), ps_st[g % 2][0:KV, :], ACT.Exp,
                                       scale=SCALE).then_inc(exp_ok, 1)
                        if ahead:
                            for task in tasks_at.get((b, g), ()):
                                evacuate(task, q + 1, 1 - par, bank_of[task])
                        if ahead == 0 and (b, g) == (3, 1):
                            high_part(0)
                    if ahead == 0 and b == 3:
                        act.activation(gelu_warm[:], tanh_g[:, 0:1], ACT.Gelu)
                    act.wait_ge(o_ps, t + 1)
                    act.activation(att_t[:].rearrange("p a s -> p (a s)"), ps_o[:, 0:2 * S], ACT.Copy) \
                        .then_inc(o_ok, 1)

            quads(act, step)

            def gelus(q, par):
                for c in range(FC):
                    act.wait_ge(up_ps, FC * q + c + 1)
                    act.activation(act_h[par][:, c, :], up_banks[c][:], ACT.Gelu).then_inc(gelu_ok, 1)

            def square(q, par):
                act.wait_ge(sqsum_ok, SUM0 + q)
                for c in range(FC):
                    act.wait_ge(gelu_ok, GELU0 + FC * q + c + 1)
                    act.activation(squares[:, c, :], act_h[par][:, c, :], ACT.Square).then_inc(sq_ok, 1)

            gelus(0, 0)
            high_part(1)
            square(0, 0)

            def stage(k, par, ahead):
                q = 2 * k + par
                if ahead:
                    gelus(q + 1, 1 - par)
                if ahead == 2:
                    high_part(q + 2)
                if ahead:
                    square(q + 1, 1 - par)
                act.wait_ge(down_ps, q + 1)
                act.activation(ffn_t[:], ps_o[:], ACT.Copy, scale=tanh_g[:, 1:2]).then_inc(ft_ok, 1)

            quads(act, stage)

        @block.tensor
        def _(pe):
            def warm_up(n):
                for _ in range(n):
                    pe.matmul(ps_p[1][:, 0:128], ident[:], ident[:], start=True, stop=True)

            pe.wait_ge(ident_ok, 1)
            warm_up(3)
            pe.wait_ge(maskf_ok, 1)
            pe.transpose(ps_o[0:KV, 0:B], mask_rows_f[:], ident[0:B, 0:B]).then_inc(maskt_ps, 1)
            pe.wait_ge(valid_ok, 1)
            pe.wait_ge(ones_ok, 1)
            pe.matmul(ps_t[0:KV, 0:B], ones[0:KV, 0:KV], valid[:], start=True, stop=True).then_inc(count_ps, 1)
            warm_up(6)
            pe.wait_ge(ld_w, 48)
            for n in range(3):
                if n == 2:
                    pe.wait_ge(wt_ok, 1)
                pe.transpose(ps_s[n % 2][:, 0:D], w_raw[:, n, :], ident[:]).then_inc(wt_ps, 1)

            def prepare(task, k, par, first=False):
                q = 2 * k + par
                bank = (first_bank_of if first else bank_of)[task]
                if first and task in (KP, QP):
                    pe.wait_ge(wt_ok, 3)
                if task == XT:
                    pe.wait_ge(xn_ok, NB * (q + 1))
                    for b in range(NB):
                        mm = pe.transpose(bank[:, b * S:(b + 1) * S], xn[:, b, :], ident[:])
                    mm.then_inc(xt_ps, 1)
                elif task == CT:
                    if not first:
                        pe.wait_ge(v_ok, (G + 2) * q)
                    pe.wait_ge(fill_ok, NB * (q + 1) + 1)
                    pe.wait_ge(ld_ctx[par], 16 * (k + 1))
                    for b in range(NB):
                        mm = pe.matmul(bank[:, b * KV:(b + 1) * KV], context_in[:, par, b, :], fill[:, b, :],
                                       start=True, stop=True)
                    mm.then_inc(ct_ps, 1)
                elif task == QP:
                    pe.wait_ge(xt_ok, q + 1)
                    pe.matmul(bank[:], w_t[:, 0, :], xn_t[:], start=True, stop=True).then_inc(q_ps, 1)
                elif task == KP:
                    pe.wait_ge(ct_ok, q + 1)
                    pe.matmul(bank[:, 0:NB * KV], w_t[:, 1, :], context_t[:].rearrange("p b k -> p (b k)"),
                              start=True, stop=True).then_inc(k_ps, 1)
                elif task == VP:
                    pe.wait_ge(ct_ok, q + 1)
                    if first:
                        pe.wait_ge(krows_ok, G)
                    else:
                        pe.wait_ge(qrows_ok, G * (q + 1))
                    for b in range(NB):
                        mm = pe.matmul(bank[0:KV, b * D:(b + 1) * D], context_t[:, b, :], w_t[:, 2, :],
                                       start=True, stop=True)
                    mm.then_inc(v_ps, 1)
                elif task in KR:
                    g = KR.index(task)
                    if g == 0:
                        pe.wait_ge(sel_ok, 1)
                        pe.wait_ge(khi_ok, q + 1)
                        pe.wait_ge(klo_ok, q + 1)
                    elif not first:
                        if g == 1:
                            pe.wait_ge(qrows_ok, G * q + 1)
                        else:
                            pe.wait_ge(krows_ok, G * q + g - 1)
                    pe.matmul(bank[:, 0:NB * KV], select["k_hi_sel"][:, g, :], k_hi[:], start=True, stop=False)
                    pe.matmul(bank[:, 0:NB * KV], select["k_lo_sel"][:, g, :], k_lo[:], start=False, stop=True) \
                        .then_inc(krows_ps, 1)
                else:
                    g = QR.index(task)
                    if g == 0:
                        pe.wait_ge(sel_ok, 1)
                        pe.wait_ge(qhi_ok, q + 1)
                        pe.wait_ge(qlo_ok, q + 1)
                    if first:
                        pass
                    elif g == 3:
                        pe.wait_ge(qrows_ok, G * q + 2)
                    elif g:
                        pe.wait_ge(krows_ok, G * q + g + 2)
                    pe.matmul(bank[:], select["q_hi_sel"][:, g, :], q_hi[:], start=True, stop=False)
                    pe.matmul(bank[:], select["q_lo_sel"][:, g, :], q_lo[:], start=False, stop=True) \
                        .then_inc(qrows_ps, 1)

            def scores(t, b, par, g, first=False):
                if g >= 2 or not first:
                    pe.wait_ge(max_ok, G * t + g - 1)
                pe.matmul(ps_s[g % 2][:, 0:J * KV], q_rows[par][:, g, b * S:(b + 1) * S],
                          k_slots[b // 2][:, g, :, b % 2, :], start=True, stop=True).then_inc(s_ps, 1)

            def shifted(t, b, par, g):
                pe.wait_ge(exp_ok, EXP0 + G * t + g - 1)
                pe.wait_ge(max_ok, G * t + g + 1)
                bank = ps_st[g % 2][0:KV, :]
                pe.matmul(bank, k_rows[par][:, g, b, :], q_slots[b // 2][:, g, :, b % 2, :], start=True, stop=False)
                for j in range(J):
                    mm = pe.matmul(bank[:, j * S:(j + 1) * S],
                                   neg_max[:, b % 2, J * g + j:J * g + j + 1].to_broadcast([S, KV]),
                                   ident_b[:], start=False, stop=(j == J - 1))
                mm.then_inc(st_ps, 1)

            def products(t, q, b, par, g):
                pe.wait_ge(exp_ok, EXP0 + G * t + g + 1)
                if g == 0:
                    pe.wait_ge(o_ok, O0 + t)
                    if b == 0:
                        pe.wait_ge(v_ok, (G + 2) * (q + 1))
                half_of = slice(0, S) if g < 3 else slice(S, 2 * S)
                for j in range(J):
                    mm = pe.matmul(ps_o[32 * j:32 * j + 32, half_of], v_blocks[par][:, b, J * g + j, :],
                                   probs[:, g, j, :], start=(g in (0, 3)), stop=(g in (2, 3)))
                if g == 3:
                    mm.then_inc(o_ps, 1)

            def turn_back(t):
                pe.wait_ge(o_ok, O0 + t)
                pe.wait_ge(x2_ok, X20 + t)
                for n in range(2):
                    mm = pe.transpose(ps_t[:, n * S:(n + 1) * S], att_t[:, n, :], ident[:])
                mm.then_inc(t_ps, 1)

            for task in first_tasks:
                prepare(task, 0, 0, first=True)
            warm_up(13)
            pe.wait_ge(qrows_ok, G)
            pe.wait_ge(kslots_ok[0], 16 * J)
            for g in range(G):
                scores(0, 0, 0, g, first=True)
                warm_up(1)
            pe.wait_ge(ident_b_ok, 1)
            pe.wait_ge(share_ok, 1)

            def turn_y(q):
                pe.wait_ge(y_ok, NB * (q + 1))
                for b in range(NB):
                    mm = pe.transpose(ps_p[0][:, b * S:(b + 1) * S], y[:, b, :], ident[:])
                mm.then_inc(yt_ps, 1)

            def step(k, par, ahead):
                q = 2 * k + par
                for b in range(NB):
                    t = NB * q + b
                    if ahead == 0 and b == 0:
                        pe.wait_ge(abs_ok, 2)
                        pe.matmul(ps_p[1][:, 0:2], ones[:], abs_sum[:], start=True, stop=True).then_inc(abs_ps, 1)
                    if b % 2 == 0:
                        pe.wait_ge(qslots_ok[b // 2], 16 * J * (q + 1))
                    for g in range(G):
                        shifted(t, b, par, g)
                        if g == 2:
                            products(t, q, b, par, 0)
                            products(t, q, b, par, 1)
                        if g == 1:
                            turn_back(t)
                        if b < 3:
                            if b == 1 and g == 0:
                                pe.wait_ge(kslots_ok[1], 16 * J * (q + 1))
                            scores(t + 1, b + 1, par, g)
                        elif ahead:
                            if g == 0:
                                pe.wait_ge(qrows_ok, G * (q + 2))
                                pe.wait_ge(kslots_ok[0], 16 * J * (q + 2))
                            scores(t + 1, 0, 1 - par, g)
                        if ahead:
                            for task in tasks_at.get((b, g), ()):
                                prepare(task, k + par, 1 - par)
                        if ahead == 0 and (b, g) == (2, 3):
                            pe.wait_ge(tern_ok, 2)
                            for n in range(2):
                                for c in range(FC):
                                    mm = pe.transpose(ps_p[n][:, c * 128:(c + 1) * 128],
                                                      tern[:, n, c * 128:(c + 1) * 128], ident[:])
                                mm.then_inc(ternt_ps, 1)
                        if ahead == 0 and (b, g) == (3, 1):
                            pe.wait_ge(ternt_ok, 2)
                            turn_y(0)
                    products(t, q, b, par, 2)
                    products(t, q, b, par, 3)

            quads(pe, step)

            def up(q):
                pe.wait_ge(yhi_ok, q + 1)
                pe.wait_ge(ylo_ok, q + 1)
                for c in range(FC):
                    w = wu_t[:, c * 128:(c + 1) * 128]
                    pe.wait_ge(gelu_ok, FC * q + c + 1)
                    pe.matmul(up_banks[c][:], w, y_hi[:], start=True, stop=False)
                    pe.matmul(up_banks[c][:], w, y_lo[:], start=False, stop=True).then_inc(up_ps, 1)

            def sum_squares(b, par):
                return pe.matmul(ps_p[1][:, b:b + 1], square_sum[:, par, b * S:(b + 1) * S],
                                 ones[:, 0:1], start=True, stop=True)

            def down(q, par, last=False):
                pe.wait_ge(ft_ok, FT0 + q)
                for c in range(FS, FC):
                    pe.wait_ge(gelu_ok, GELU0 + FC * q + c + 1)
                    pe.matmul(ps_o[:], wd_t[:, c, :].bitcast(F32), act_h[par][:, c, :], start=(c == FS), stop=False)
                pe.wait_ge(sqsum_ok, SUM0 + q + 1)
                pe.wait_ge(meansq_ok, MEANSQ0 + q)
                if last:
                    for b in range(NB):
                        mm = sum_squares(b, par)
                    mm.then_inc(ssq_ps, 1)
                for c in range(FS):
                    pe.wait_ge(hhi_ok, FS * q + c + 1)
                    pe.matmul(ps_o[:], wd_t[:, c, :], h_hi[par][:, c, :], start=False, stop=False)
                    pe.wait_ge(hlo_ok, FS * q + c + 1)
                    mm = pe.matmul(ps_o[:], wd_t[:, c, :], h_lo[par][:, c, :], start=False, stop=(c == FS - 1))
                    if c < FS - 1 and not last:
                        sum_squares(c, par)
                mm.then_inc(down_ps, 1)
                if not last:
                    for b in range(FS - 1, NB):
                        mm = sum_squares(b, par)
                    mm.then_inc(ssq_ps, 1)

            def turn_out(q):
                pe.wait_ge(ft_ok, FT0 + q + 1)
                pe.wait_ge(res_ok, RES0 + NB * q)
                for b in range(NB):
                    mm = pe.transpose(ps_t[:, b * D:(b + 1) * D], ffn_t[:, b * S:(b + 1) * S], ident[:])
                mm.then_inc(back_ps, 1)

            up(0)
            turn_back(B)
            turn_y(1)

            def stage(k, par, ahead):
                q = 2 * k + par
                if ahead:
                    up(q + 1)
                if ahead == 2:
                    turn_y(q + 2)
                down(q, par, last=(ahead == 0))
                turn_out(q)

            quads(pe, stage)

        @block.vector
        def _(dve):
            dve.wait_ge(ld_masks, 16)
            dve.tensor_copy(mask_rows_f[:], mask_rows[:]).then_inc(maskf_ok, 1)

            def ahead_of(k, par, piece, q_before=True):
                q = 2 * k + par
                if piece == 0:
                    dve.wait_ge(ld_mask, 16 * (q + 1))
                    dve.tensor_scalar(invalid[:].rearrange("p b k -> p (b k)"), mask_in[:], 0.0, None, ALU.is_equal) \
                        .then_inc(invalid_ok, 1)
                elif piece == 1:
                    dve.wait_ge(ld_x[par], 16 * (k + 1))
                    for b in range(NB):
                        dve.bn_stats(stats[:, b, :], xs[:, q * NB + b + 1, :]).then_inc(stats_ok, 1)
                elif piece in (2, 3):
                    if q_before:
                        dve.wait_ge(xt_ps, q)
                        dve.wait_ge(ct_ps, q)
                    dve.wait_ge(invalid_ok, q + 1)
                    dve.wait_ge(stats_ok, NB * (q + 1))
                    for b in range(2 * piece - 4, 2 * piece - 2):
                        dve.wait_ge(diag_ok, NB * q + b + 1)
                        dve.scalar_tensor_tensor(out=fill[:, b, :], in0=invalid[:, b, :],
                                                 scalar=valid_share[:, bass.ds(q * NB + b, 1)], in1=diag[:, b, :],
                                                 op0=ALU.mult, op1=ALU.add).then_inc(fill_ok, 1)
                elif piece == 4:
                    for b in range(NB):
                        dve.bn_aggr(moments[:, b, :], stats[:, b, :]).then_inc(moments_ok, 1)
                    dve.wait_ge(moments_ok, NB * (q + 1))
                    dve.tensor_scalar(var_eps[:], moments[:, :, 1], LN_EPS, None, ALU.add).then_inc(vareps_ok, 1)
                else:
                    dve.wait_ge(rstd_ok, q + 1)
                    for b in range(2 * piece - 10, 2 * piece - 8):
                        dve.tensor_scalar(xn[:, b, :], xs[:, q * NB + b + 1, :], moments[:, b, 0:1],
                                          rstd[:, b:b + 1], ALU.subtract, ALU.mult).then_inc(xn_ok, 1)

            piece_at = {(1, 1): 0, (1, 2): 1, (1, 3): 2, (2, 0): 4, (2, 1): 3, (2, 2): 5, (2, 3): 6}

            def evacuate(task, q, par, bank):
                if task == QP:
                    dve.wait_ge(qhi_ok, q + 1)
                    dve.scalar_tensor_tensor(out=q_lo[:], in0=bank[:], scalar=q_bias[:, 0:1],
                                             in1=q_hi[:].bitcast(F32), op0=ALU.add, op1=ALU.subtract) \
                        .then_inc(qlo_ok, 1)
                elif task == KP:
                    dve.wait_ge(khi_ok, q + 1)
                    dve.scalar_tensor_tensor(out=k_lo[:], in0=bank[:, 0:NB * KV], scalar=k_bias[:, 0:1],
                                             in1=k_hi[:].bitcast(F32), op0=ALU.add, op1=ALU.subtract) \
                        .then_inc(klo_ok, 1)
                elif task == VP:
                    dve.wait_ge(v_ps, q + 1)
                    dve.wait_ge(vzero_ok, par + 1)
                    keep = valid[:, bass.ds(q * NB, NB)]
                    for g in range(G):
                        dve.tensor_tensor(v_store[par][0:KV, :, J * g:J * g + J, (g % 3) * HD:(g % 3 + 1) * HD],
                                          bank[0:KV].rearrange("p (b g j i) -> p b g j i", b=NB, g=G, j=J)[:, :, g],
                                          keep.rearrange("p (b o n) -> p b o n", o=1, n=1).to_broadcast([KV, NB, J, HD]),
                                          ALU.mult).then_inc(v_ok, 1)
                    dve.tensor_copy(bass.AP(v_store[par], 24, [[NB * H * VC, KV], [H * VC, NB], [J * VC + 1, 3], [VC, J]]),
                                    keep.rearrange("p (b o n) -> p b o n", o=1, n=1).to_broadcast([KV, NB, 3, J])) \
                        .then_inc(v_ok, 1)
                    dve.tensor_copy(v_blocks[par][:, :, 12:16, 24],
                                    keep.rearrange("p (b o) -> p b o", o=1).to_broadcast([KV, NB, J])) \
                        .then_inc(v_ok, 1)

            def maximum(t, b, g):
                dve.wait_ge(s_ps, G * t + g + 1)
                dve.tensor_reduce(neg_max[:, b % 2, J * g:J * g + J],
                                  ps_s[g % 2][:, 0:J * KV].rearrange("p (j k) -> p j k", j=J),
                                  AX.X, ALU.max, negate=True).then_inc(max_ok, 1)

            def finish(t):
                tb = ps_t[:]
                dve.wait_ge(t_ps, t + 1)
                first = tb[:, 0:128].rearrange("p (j c) -> p j c", j=J)
                second = tb[:, 128:256].rearrange("p (j c) -> p j c", j=J)
                dve.reciprocal(inv_den[:, 0:12].rearrange("p (a j) -> p a j", a=3),
                               first[:, :, 24:27].rearrange("p j a -> p a j")).then_inc(den_ok, 1)
                dve.reciprocal(inv_den[:, 12:16], second[:, :, 24]).then_inc(den_ok, 1)
                dve.wait_ge(den_ok, 2 * t + 1)
                dve.tensor_tensor(att[:, 0:96].rearrange("p (a j i) -> p a j i", a=3, j=J),
                                  first[:, :, 0:24].rearrange("p j (a i) -> p a j i", a=3),
                                  inv_den[:, 0:12].rearrange("p (a j o) -> p a j o", a=3, o=1)
                                  .to_broadcast([S, 3, J, HD]), ALU.mult).then_inc(att_ok, 1)
                dve.wait_ge(den_ok, 2 * t + 2)
                dve.tensor_tensor(att[:, 96:128].rearrange("p (j i) -> p j i", j=J), second[:, :, 0:HD],
                                  inv_den[:, 12:16].rearrange("p (j o) -> p j o", o=1).to_broadcast([S, J, HD]),
                                  ALU.mult).then_inc(att_ok, 1)
                dve.wait_ge(att_ok, 2 * t + 2)
                dve.tensor_tensor(xs[:, t, :], xs[:, t, :], att[:], ALU.add).then_inc(x2_ok, 1)

            def measure(t):
                dve.bn_stats(stats2[:, t], xs[:, t, :]).then_inc(stats2_ok, 1)

            dve.wait_ge(maskt_ps, 1)
            dve.tensor_scalar(valid[:], ps_o[0:KV, 0:B], 0.0, None, ALU.not_equal).then_inc(valid_ok, 1)
            dve.memset(var2[:], 0.0).then_inc(fill_ok, 1)
            ahead_of(0, 0, 1)
            dve.wait_ge(count_ps, 1)
            dve.tensor_scalar(valid_n[:], ps_t[0:KV, 0:B], 1.0, None, ALU.max).then_inc(count_ok, 1)
            dve.wait_ge(stats_ok, NB)
            ahead_of(0, 0, 4)
            dve.wait_ge(count_ok, 1)
            dve.reciprocal(valid_share[:], valid_n[:]).then_inc(count_ok, 1)
            dve.wait_ge(count_ok, 2)
            dve.wait_ge(valid_ok, 1)
            dve.tensor_tensor(valid_share[:], valid_share[:], valid[:], ALU.mult).then_inc(share_ok, 1)
            ahead_of(0, 0, 0)
            dve.wait_ge(share_ok, 1)
            ahead_of(0, 0, 2, q_before=False)
            ahead_of(0, 0, 3, q_before=False)
            ahead_of(0, 0, 5)
            ahead_of(0, 0, 6)
            dve.wait_ge(sel_zero, 4)
            dve.wait_ge(ident_ok, 1)
            parts = {"q_hi_sel": (0, 1), "q_lo_sel": (2, 3), "k_hi_sel": (0, 2), "k_lo_sel": (1, 3)}
            for n, cs in parts.items():
                for c in cs:
                    last = dve.tensor_copy(
                        select[n][:].rearrange("p g (j c i) -> p g j c i", j=J, c=C)[:, :, :, c, :],
                        ident[:].rearrange("p (g j i) -> p g j i", g=G, j=J))
            last.then_inc(sel_ok, 1)
            evacuate(KP, 0, 0, first_bank_of[KP])
            evacuate(QP, 0, 0, first_bank_of[QP])
            for g in (1, 3):
                dve.wait_ge(krows_ps, g + 1)
                dve.tensor_copy(k_rows[0][:, g].rearrange("p b k -> p (b k)"), first_bank_of[KR[g]][:, 0:NB * KV]) \
                    .then_inc(krows_ok, 1)
            for g in (1, 3):
                dve.wait_ge(qrows_ps, g + 1)
                dve.tensor_copy(q_rows[0][:, g, :], first_bank_of[QR[g]][:]).then_inc(qrows_ok, 1)
            evacuate(VP, 0, 0, first_bank_of[VP])
            dve.wait_ge(tanh_ok, 1)
            dve.wait_ge(ld_bias, 48)
            dve.tensor_scalar(gated_bias[:], v_bias[:], tanh_g[:, 0:1], None, ALU.mult).then_inc(gbias_ok, 1)
            dve.tensor_copy(ident_b[:], ident[:]).then_inc(ident_b_ok, 1)
            ahead_of(0, 1, 0)
            ahead_of(0, 1, 1)
            dve.wait_ge(stats_ok, 2 * NB)
            ahead_of(0, 1, 4)
            dve.memset(inv_den[:], 0.0).then_inc(exp_ok, EXP0)
            dve.memset(mean_gap[:], 0.0).then_inc(gelu_ok, GELU0)
            dve.memset(xs[:, 0, :], 0.0).then_inc(x2_ok, X20)
            for g in range(2):
                maximum(0, 0, g)
            dve.wait_ge(xt_ps, 1)
            ahead_of(0, 1, 5)
            ahead_of(0, 1, 6)
            for g in range(2, G):
                maximum(0, 0, g)
            ahead_of(0, 1, 2)
            ahead_of(0, 1, 3)
            dve.wait_ge(x2_ok, X20)

            raws = [wu_raw[:].rearrange("p c d -> p (c d)"), wd_raw[:]]

            def weight_sums():
                dve.wait_ge(ld_ffn, 32)
                for n in range(2):
                    dve.tensor_reduce(abs_sum[:, n:n + 1], raws[n], AX.X, ALU.add, apply_absolute_value=True) \
                        .then_inc(abs_ok, 1)

            def weights_below():
                dve.wait_ge(abs_ps, 1)
                dve.tensor_scalar(thresh[:], ps_p[1][:, 0:2], 1.0 / (F * D), 0.5, ALU.mult, ALU.mult).then_inc(thresh_ok, 1)
                dve.tensor_scalar(neg_thresh[:], ps_p[1][:, 0:2], 1.0 / (F * D), -0.5, ALU.mult, ALU.mult) \
                    .then_inc(thresh_ok, 1)
                dve.wait_ge(thresh_ok, 2)
                for n in range(2):
                    dve.tensor_scalar(tern_neg[:, n, :], raws[n], neg_thresh[:, n:n + 1], None, ALU.is_lt).then_inc(neg_ok, 1)

            def ternary_weights(n):
                dve.wait_ge(neg_ok, n + 1)
                dve.scalar_tensor_tensor(out=tern[:, n, :], in0=raws[n], scalar=thresh[:, n:n + 1],
                                         in1=tern_neg[:, n, :], op0=ALU.is_gt, op1=ALU.subtract) \
                    .then_inc(tern_ok, 1)

            def moments_of(n):
                cols = SEGMENTS[n]
                dve.wait_ge(stats2_ok, cols.stop)
                even, odd = stats2[:, cols, 0], stats2[:, cols, 1]
                dve.tensor_tensor(mean2[:, cols], even[:, :, 1], odd[:, :, 1], ALU.add).then_inc(moments2_ok, 1)
                dve.tensor_tensor(mean_gap[:, cols], even[:, :, 1], odd[:, :, 1], ALU.subtract).then_inc(moments2_ok, 1)
                dve.tensor_tensor(var2[:, cols], even[:, :, 2], odd[:, :, 2], ALU.add).then_inc(moments2_ok, 1)
                dve.wait_ge(moments2_ok, 5 * n + 3)
                dve.tensor_scalar(mean2[:, cols], mean2[:, cols], 0.5, None, ALU.mult).then_inc(gap_ok, 1)
                dve.scalar_tensor_tensor(out=mean_gap[:, cols], in0=mean_gap[:, cols], scalar=0.25,
                                         in1=mean_gap[:, cols], op0=ALU.mult, op1=ALU.mult).then_inc(gap_ok, 1)
                dve.wait_ge(gap_ok, 2 * n + 2)
                dve.scalar_tensor_tensor(out=var2[:, cols], in0=var2[:, cols], scalar=1.0 / D, in1=mean_gap[:, cols],
                                         op0=ALU.mult, op1=ALU.add).then_inc(moments2_ok, 1)
                dve.wait_ge(moments2_ok, 5 * n + 4)
                dve.tensor_scalar(var2_eps[:, cols], var2[:, cols], LN_EPS, None, ALU.add).then_inc(moments2_ok, 1)

            def scales_of(n):
                cols = SEGMENTS[n]
                dve.wait_ge(root_ok, 2 * n + 2)
                dve.scalar_tensor_tensor(out=ffn_den[:, cols], in0=root_eps[:, cols], scalar=RMS_EPS,
                                         in1=root[:, cols], op0=ALU.mult, op1=ALU.add).then_inc(den2_ok, 1)
                dve.wait_ge(den2_ok, n + 1)
                dve.reciprocal(ffn_scale[:, cols], ffn_den[:, cols]).then_inc(scale2_ok, 1)

            def norm(q):
                for b in range(NB):
                    dve.tensor_scalar(y[:, b, :], xs[:, q * NB + b + 1, :],
                                      mean2[:, bass.ds(q * NB + b + 1, 1)], ffn_scale[:, bass.ds(q * NB + b + 1, 1)],
                                      ALU.subtract, ALU.mult).then_inc(y_ok, 1)

            def low_part(q):
                dve.wait_ge(yhi_ok, q + 1)
                dve.tensor_tensor(y_lo[:], ps_p[0][:], y_hi[:].bitcast(F32), ALU.subtract).then_inc(ylo_ok, 1)

            def step(k, par, ahead):
                q = 2 * k + par
                for b in range(NB):
                    t = NB * q + b
                    for g in range(G):
                        if g == 2:
                            dve.wait_ge(x2_ok, X20 + t + 1)
                        if b < 3 or ahead:
                            maximum(t + 1, b + 1, g)
                        if g == 2:
                            measure(t)
                        if ahead == 1 and (b, g) == (1, 2):
                            moments_of(0)
                        if ahead == 1 and (b, g) == (2, 2):
                            weight_sums()
                        if ahead == 0 and (b, g) == (0, 3):
                            weights_below()
                        if ahead == 0 and (b, g) == (1, 2):
                            ternary_weights(0)
                        if ahead == 0 and (b, g) == (2, 0):
                            ternary_weights(1)
                        if ahead == 0 and (b, g) == (1, 0):
                            moments_of(1)
                        if ahead == 0 and (b, g) == (2, 1):
                            scales_of(0)
                        if ahead == 0 and (b, g) == (2, 2):
                            scales_of(1)
                        if ahead == 0 and (b, g) == (2, 3):
                            dve.wait_ge(scale2_ok, 1)
                            norm(0)
                        if ahead == 0 and (b, g) == (3, 1):
                            low_part(0)
                        if ahead == 0 and (b, g) == (3, 2):
                            dve.wait_ge(yt_ps, 1)
                            norm(1)
                        if ahead == 2 and (b, g) in piece_at:
                            ahead_of(k + 1, par, piece_at[b, g])
                        if ahead:
                            for task in tasks_at.get((b, g), ()):
                                evacuate(task, q + 1, 1 - par, bank_of[task])
                        if g == 1:
                            if b == 1:
                                dve.wait_ge(xb_ok, q + 1)
                            finish(t)

            quads(dve, step)
            dve.memset(thresh[:], 0.0).then_inc(sqsum_ok, SUM0)
            dve.memset(rms_inv[:], 0.0).then_inc(res_ok, RES0)
            dve.memset(mean_sq[:], 0.0).then_inc(meansq_ok, MEANSQ0)
            dve.memset(neg_thresh[:], 0.0).then_inc(ft_ok, FT0)
            finish(B)

            def high_parts(q, par):
                for c in range(FS):
                    dve.wait_ge(gelu_ok, GELU0 + FC * q + c + 1)
                    dve.tensor_copy(h_hi[par][:, c, :], act_h[par][:, c, :]).then_inc(hhi_ok, 1)

            def add_squares(q, par):
                for n in range(2):
                    dve.wait_ge(sq_ok, FC * q + 2 * n + 2)
                    dve.tensor_tensor(pair_sum[:, n, :], squares[:, 2 * n, :], squares[:, 2 * n + 1, :], ALU.add) \
                        .then_inc(pairs_ok, 1)
                dve.wait_ge(pairs_ok, 2 * q + 2)
                dve.tensor_tensor(square_sum[:, par, :], pair_sum[:, 0, :], pair_sum[:, 1, :], ALU.add) \
                    .then_inc(sqsum_ok, 1)

            high_parts(0, 0)
            low_part(1)
            dve.wait_ge(x2_ok, X20 + B + 1)
            measure(B)
            moments_of(2)
            dve.wait_ge(yt_ps, 2)
            norm(2)
            add_squares(0, 0)
            scales_of(2)
            high_parts(1, 1)
            low_part(2)
            add_squares(1, 1)
            dve.wait_ge(scale2_ok, 3)

            def mean_squares(q):
                dve.wait_ge(ssq_ps, q + 1)
                dve.tensor_scalar(mean_sq[:], ps_p[1][:, 0:NB], 1.0 / F, None, ALU.mult) \
                    .then_inc(meansq_ok, 1)

            def stage(k, par, ahead):
                q = 2 * k + par
                if ahead:
                    mean_squares(q)
                if ahead == 3:
                    dve.wait_ge(yt_ps, q + 3)
                    norm(q + 3)
                if ahead >= 2:
                    high_parts(q + 2, par)
                dve.wait_ge(rmse_ok, q + 1)
                if ahead == 0:
                    dve.wait_ge(res_ok, RES0 + NB * q)
                dve.reciprocal(rms_inv[:], rms_eps[:]).then_inc(rinv_ok, 1)
                dve.wait_ge(rinv_ok, q + 1)
                if ahead == 1:
                    mean_squares(q + 1)
                dve.wait_ge(back_ps, q + 1)
                for b in range(NB):
                    dve.scalar_tensor_tensor(out=xs[:, q * NB + b + 1, :], in0=ps_t[:, b * D:(b + 1) * D],
                                             scalar=rms_inv[:, b:b + 1], in1=xs[:, q * NB + b + 1, :],
                                             op0=ALU.mult, op1=ALU.add).then_inc(res_ok, 1)
                if ahead == 3:
                    low_part(q + 3)
                if ahead >= 2:
                    add_squares(q + 2, par)

            quads_deep(dve, stage)


_INS = ["x", "ctx_1024", "mask_Bx1x1xS2_ik0", "g_xattn", "g_ffn", "L0_xattn_Wq", "L0_xattn_bq", "L0_xattn_Wk",
        "L0_xattn_bk", "L0_xattn_Wv", "L0_xattn_bv", "L0_ffn_w_up", "L0_ffn_w_down"]


def kernel(**inputs):
    import numpy as np
    import concourse.bacc as bacc
    from concourse.bass_utils import run_bass_kernel_spmd

    nc = bacc.Bacc("TRN2", target_bir_lowering=False, num_devices=1)
    arrays, args = {}, []
    for name in _INS:
        a = np.ascontiguousarray(inputs[name])
        if name.startswith("mask"):
            a = a.reshape(B, KV)
        arrays[f"in_{name}"] = a
        args.append(nc.dram_tensor(f"in_{name}", a.shape, mybir.dt.from_np(a.dtype), kind="ExternalInput").ap())
    out = nc.dram_tensor("out_0", (B, S, D), F32, kind="ExternalOutput").ap()
    flamingo_kernel(nc, *args, out)
    r = run_bass_kernel_spmd(nc, [arrays], core_ids=[0])
    return r.results[0]["out_0"]
```
